# Optimizing a Trainium2 kernel written in Bass

```python
import numpy as np
import jax
import jax.numpy as jnp

def _softmax(x, axis=-1):
    return jax.nn.softmax(x, axis=axis)

def _gelu(x):
    return jax.nn.gelu(x, approximate=True)

def _silu(x):
    return jax.nn.silu(x)

def _sigmoid(x):
    return jax.nn.sigmoid(x)

def _layernorm(x, axis=-1, eps=1e-05):
    m = jnp.mean(x, axis=axis, keepdims=True)
    v = jnp.var(x, axis=axis, keepdims=True)
    return (x - m) / jnp.sqrt(v + eps)

def _scatter_add(tgt, idx, src, axis=0):
    return tgt.at[idx].add(src)

def _segment_sum(src, seg, n):
    return jax.ops.segment_sum(src, seg, n)
kernel_name = 'mk_xattn_ffn_d1_seqx_r8_928edb'

def setup_inputs(seed: int=0):
    np.random.seed(seed)
    _w = jnp.asarray

    def _rec_inputs():
        import jax
        import jax.numpy as jnp
        _rk = jax.random.key(seed)
        x = 7.22e-05 + 1 * jax.random.normal(jax.random.fold_in(_rk, 1), (4, 256, 512), jnp.float32)
        _lenS = 256 - jax.random.randint(jax.random.fold_in(_rk, 7), (4,), 0, max(1, 256 // 4) + 1, jnp.int32)
        _lenS2 = 1601 - jax.random.randint(jax.random.fold_in(_rk, 8), (4,), 0, max(1, 1601 // 4) + 1, jnp.int32)
        _ctx_4096P = jax.random.normal(jax.random.fold_in(_rk, 11), (4, 16, 512), jnp.float32)
        _ctx_4096c = jax.random.dirichlet(jax.random.fold_in(_rk, 511), 0.3 * jnp.ones((16,), jnp.float32), (4, 1601))
        _ctx_4096t = jnp.einsum('bsk,bkd->bsd', _ctx_4096c, _ctx_4096P)
        _ctx_4096t = _ctx_4096t * jax.lax.rsqrt(jnp.mean(jnp.square(_ctx_4096t)) + 1e-12) * 0.953939
        ctx_4096 = 4.13588e-05 + 0.999923 * (_ctx_4096t + 0.3 * jax.random.normal(jax.random.fold_in(_rk, 611), (4, 1601, 512), jnp.float32))
        return (x, ctx_4096)
    x, ctx_4096 = _rec_inputs()

    def _L0_xattn_setup():
        import jax, jax.numpy as jnp
        import numpy as np
        DIM = 512
        NUM_HEADS = 32
        NUM_KV_HEADS = 8
        HEAD_DIM = DIM // NUM_HEADS
        KV_DIM = DIM // (NUM_HEADS // NUM_KV_HEADS)
        B, S = (1, 256)
        key = jax.random.key(seed)
        ks = jax.random.split(key, 7)
        w_scale = DIM ** (-0.5)
        return {'query': jax.random.normal(ks[0], (B, S, DIM), jnp.float32), 'key': jax.random.normal(ks[1], (B, S, DIM), jnp.float32), 'value': jax.random.normal(ks[2], (B, S, DIM), jnp.float32), 'Wq': jax.random.normal(ks[3], (DIM, DIM), jnp.float32) * w_scale, 'Wk': jax.random.normal(ks[4], (DIM, KV_DIM), jnp.float32) * w_scale, 'Wv': jax.random.normal(ks[5], (DIM, KV_DIM), jnp.float32) * w_scale, 'Wo': jax.random.normal(ks[6], (DIM, DIM), jnp.float32) * w_scale}
    _L0_xattn_all = _L0_xattn_setup()
    _L0_xattn_in = {k: v for k, v in _L0_xattn_all.items() if k in ('Wq', 'Wk', 'Wv', 'Wo')}
    del _L0_xattn_all

    def _L0_ffn_setup():
        import jax, jax.numpy as jnp
        import numpy as np
        NUM_EXPERTS = 16
        TOP_K = 2
        INTER = 56
        key = jax.random.key(seed)
        k1, k2, k3, k4, k5 = jax.random.split(key, 5)
        B, S, H = (4, 256, 512)
        scale = 0.02
        return {'hid': jax.random.normal(k1, (B, S, H), dtype=jnp.float32), 'gate_w': jax.random.normal(k2, (NUM_EXPERTS, H), dtype=jnp.float32) * scale, 'u': jax.random.normal(k3, (NUM_EXPERTS * INTER, H), dtype=jnp.float32) * scale, 'g': jax.random.normal(k4, (NUM_EXPERTS * INTER, H), dtype=jnp.float32) * scale, 'd': jax.random.normal(k5, (H, NUM_EXPERTS * INTER), dtype=jnp.float32) * scale}
    _L0_ffn_all = _L0_ffn_setup()
    _L0_ffn_in = {k: v for k, v in _L0_ffn_all.items() if k in ('gate_w', 'u', 'g', 'd')}
    del _L0_ffn_all
    return {'x': x, 'ctx_4096': ctx_4096, 'L0_xattn_Wq': _L0_xattn_in['Wq'], 'L0_xattn_Wk': _L0_xattn_in['Wk'], 'L0_xattn_Wv': _L0_xattn_in['Wv'], 'L0_xattn_Wo': _L0_xattn_in['Wo'], 'L0_ffn_gate_w': _L0_ffn_in['gate_w'], 'L0_ffn_u': _L0_ffn_in['u'], 'L0_ffn_g': _L0_ffn_in['g'], 'L0_ffn_d': _L0_ffn_in['d']}

def reference(x, ctx_4096, L0_xattn_Wq, L0_xattn_Wk, L0_xattn_Wv, L0_xattn_Wo, L0_ffn_gate_w, L0_ffn_u, L0_ffn_g, L0_ffn_d):
    import jax
    import jax.numpy as jnp

    def _L0_xattn_ref(query, key, value, Wq, Wk, Wv, Wo):
        import jax, jax.numpy as jnp
        import numpy as np
        DIM = 512
        NUM_HEADS = 32
        NUM_KV_HEADS = 8
        HEAD_DIM = DIM // NUM_HEADS
        KV_DIM = DIM // (NUM_HEADS // NUM_KV_HEADS)
        B, S = (1, 256)
        b, sq, _ = query.shape
        _, sk, _ = key.shape
        rep = NUM_HEADS // NUM_KV_HEADS
        q = (query @ Wq).reshape(b, sq, NUM_HEADS, HEAD_DIM).transpose(0, 2, 1, 3)
        k = (key @ Wk).reshape(b, sk, NUM_KV_HEADS, HEAD_DIM).transpose(0, 2, 1, 3)
        v = (value @ Wv).reshape(b, sk, NUM_KV_HEADS, HEAD_DIM).transpose(0, 2, 1, 3)
        k = jnp.repeat(k, rep, axis=1)
        v = jnp.repeat(v, rep, axis=1)
        scale = HEAD_DIM ** (-0.5)
        scores = jnp.einsum('bhqd,bhkd->bhqk', q, k) * scale
        probs = jax.nn.softmax(scores, axis=-1)
        out = jnp.einsum('bhqk,bhkd->bhqd', probs, v)
        out = out.transpose(0, 2, 1, 3).reshape(b, sq, DIM)
        return out @ Wo

    def _L0_ffn_ref(hid, gate_w, u, g, d):
        import jax, jax.numpy as jnp
        import numpy as np
        NUM_EXPERTS = 16
        TOP_K = 2
        INTER = 56
        B, S, H = hid.shape
        x = hid.reshape(-1, H)
        bs = x.shape[0]
        logits = x @ gate_w.T
        probs = jax.nn.softmax(logits.astype(jnp.float32), axis=-1)
        vals, idx = jax.lax.top_k(probs, TOP_K)
        vals = vals / jnp.sum(vals, axis=-1, keepdims=True)
        rows = jnp.arange(bs)[:, None]
        w = jnp.zeros((bs, NUM_EXPERTS), dtype=jnp.float32).at[rows, idx].set(vals)
        w = w.astype(x.dtype)
        gate_out = (x @ g.T).reshape(bs, NUM_EXPERTS, INTER)
        up_out = (x @ u.T).reshape(bs, NUM_EXPERTS, INTER)
        h = jax.nn.silu(gate_out) * up_out
        d_r = d.reshape(H, NUM_EXPERTS, INTER)
        out = jnp.einsum('bei,hei,be->bh', h, d_r, w)
        return out.reshape(B, S, H)
    x = x + _L0_xattn_ref(_layernorm(x, axis=-1), ctx_4096, ctx_4096, L0_xattn_Wq, L0_xattn_Wk, L0_xattn_Wv, L0_xattn_Wo)
    x = x + _L0_ffn_ref(_layernorm(x, axis=-1), L0_ffn_gate_w, L0_ffn_u, L0_ffn_g, L0_ffn_d)
    return x

_drawn_inputs = setup_inputs


def setup_inputs(seed=0):
    import zlib

    import numpy as np

    out = dict(_drawn_inputs(seed))
    spreads = {}
    factors = {'L0_ffn_gate_w': 5.946, 'L0_ffn_u': 5.515, 'L0_ffn_g': 5.7, 'L0_ffn_d': 5.557}
    for name, (base, spread) in spreads.items():
        noise = np.random.default_rng([zlib.crc32(name.encode()), seed]).standard_normal(out[name].shape)
        drawn = base * np.exp(spread * noise) if base else spread * noise
        out[name] = jnp.asarray(drawn.astype(out[name].dtype))
    for name, factor in factors.items():
        out[name] = (out[name] * factor).astype(out[name].dtype)
    return out
```

```python
from contextlib import ExitStack

import concourse.bass as bass
from concourse import mybir

F32 = mybir.dt.float32
F32R = mybir.dt.float32r
U32 = mybir.dt.uint32
ACT = mybir.ActivationFunctionType
ALU = mybir.AluOpType
AX = mybir.AxisListType

P = 128
B, S, D = 4, 256, 512
SK = 1601
C = D // P
HEADS, KV, HD = 32, 8, 16
REP = HEADS // KV
QC = REP * S
TILES = (SK + P - 1) // P
LAST = SK - (TILES - 1) * P
GROUPS = B * KV
NQ = QC // P
PIECES = 4
PIECE = 402
STARTS = [min(i * (PIECE - 2), SK - PIECE) for i in range(PIECES)]
UNITS = NQ * PIECES
FOUR = 4
E, INTER = 16, 56
F = E * INTER
FC = F // P
EPS = 1e-5
PARTS = ((0, 0), (0, 1), (1, 0))
ZROW, MROW = 64, 96
SROWS = MROW + 2

KB = 1024
AT_IDENT, AT_EPS, AT_WORK3, AT_WO = 0, KB // 2, KB, 34 * KB
AT_RAW = 42 * KB
AT_V = 84 * KB
AT_WORK = 110 * KB


class Plan:
    pass


def k_base(nc):
    return (nc.sbuf_base + 63) // 64 * 64


def product(pe, out, lhsT, rhs, chunks, first=True, last=True):
    steps = [(p, q, c) for p, q in PARTS for c in chunks]
    for i, (p, q, c) in enumerate(steps):
        mm = pe.matmul(out, lhsT(p, c), rhs(q, c), start=first and i == 0,
                       stop=last and i == len(steps) - 1)
    return mm


def project(nc, k):
    with ExitStack() as ctx:
        base = [k_base(nc) + AT_WORK]

        def sb(name, shape, dt):
            size = 4
            for n in shape[1:]:
                size *= n
            t = nc.alloc_sbuf_tensor_at(name, shape, dt, offset=base[0])
            base[0] += (size + 63) // 64 * 64
            return t

        def sem(name):
            return ctx.enter_context(nc.semaphore(name))

        wraw = sb("wraw", [P, C, D + 2 * P], F32)
        w = [sb(f"w{n}", [P, C, D + 2 * P], F32R) for n in ("hi", "lo")]
        tok = [sb(f"tok{i}", [P, 4, D], F32) for i in range(2)]
        tokT = [[sb(f"tokT{n}{i}", [P, C, 4 * P], F32R) for n in ("hi", "lo")] for i in range(2)]
        out = [[sb(f"out{n}{i}", [P, 4 * P], F32R) for n in ("hi", "lo")] for i in range(2)]
        stats = sb("stats", [P, 8, 6], F32)
        mean_var = sb("mean_var", [P, 8, 2], F32)
        std = sb("std", [P, 8], F32)
        rstd = sb("rstd", [P, 8], F32)
        turn_bank = [k.bank[:, i, :] for i in range(4)]
        kq_bank = [k.bank[:, 4 + i, :] for i in range(2)]
        v_bank = [k.bank[:, 6 + i, :] for i in range(2)]

        w_loaded = [sem(f"w_loaded{i}") for i in range(3)]
        w_ready = sem("w_ready")
        w_hi_done = sem("w_hi_done")
        id_zero = sem("id_zero")
        id_ready = sem("id_ready")
        tok_loaded = [sem(f"tok_loaded{i}") for i in range(2)]
        stats_ready = sem("stats_ready")
        var_ready = sem("var_ready")
        eps_ready = sem("eps_ready")
        std_ready = sem("std_ready")
        rstd_ready = sem("rstd_ready")
        ln_done = sem("ln_done")
        turned = sem("turned")
        turn_hi = sem("turn_hi")
        turn_lo = sem("turn_lo")
        kq_ready = sem("kq_ready")
        kq_hi = sem("kq_hi")
        kq_lo = sem("kq_lo")
        stored = [sem(f"stored{i}") for i in range(2)]
        v_ready = sem("v_ready")
        v_free = sem("v_free")
        ffn_loaded = k.ffn_loaded

        x_tok = k.x.rearrange("b s d -> (b s) d")
        QU = 8
        X_TILES = B * S // P

        def tiles(r):
            return 4 if r < 3 else 1

        def rows(r):
            return P if r < 3 else LAST

        def first_tile(b, r):
            return X_TILES + TILES * b + 4 * r

        block = ctx.enter_context(nc.Block())

        @block.sync
        def _(sp):
            for u in range(2):
                sp.dma_start(tok[u][:], x_tok[512 * u:512 * u + 512, :].rearrange("(t p) d -> p t d", p=P)
                             ).then_inc(tok_loaded[u], 16)
                if u == 0:
                    sp.dma_start(wraw[:, :, 0:D], k.wq.rearrange("(c p) n -> p c n", p=P)).then_inc(w_loaded[0], 16)
            sp.dma_start(wraw[:, :, D:D + P], k.wk.rearrange("(c p) n -> p c n", p=P)).then_inc(w_loaded[1], 16)
            sp.dma_start(wraw[:, :, D + P:], k.wv.rearrange("(c p) n -> p c n", p=P)).then_inc(w_loaded[2], 16)

            def load(b, r):
                if isinstance(b, int) and b == 0 and r < 2:
                    sp.wait_ge(turned, 4 * (r + 1))
                elif r < 2:
                    sp.wait_ge(turned, first_tile(b - 1, r + 2) + tiles(r + 2))
                else:
                    sp.wait_ge(turned, first_tile(b, r - 2) + 4)
                src = k.ctx[bass.ds(b, 1), 512 * r:512 * r + P * (tiles(r) - 1) + rows(r), :]
                sp.dma_start(tok[r % 2][0:rows(r), 0:tiles(r), :],
                             src.rearrange("o (t p) d -> p (o t) d", p=rows(r))).then_inc(tok_loaded[r % 2], 16)

            def store_k(b, r):
                sp.wait_ge(kq_lo, QU + 4 * b + r + 1)
                n = P * (tiles(r) - 1) + rows(r)
                for part in range(2):
                    sp.dma_start(k.k_dram[part, bass.ds(P * b, P), 512 * r:512 * r + n],
                                 out[r % 2][part][:, 0:n].bitcast(F32)).then_inc(stored[r % 2], 16)

            def store_q(u):
                for m in range(C):
                    sp.wait_ge(kq_lo, 4 * u + m + 1)
                    for part in range(2):
                        dst = k.q_dram[part, 2 * D * u:2 * D * (u + 1), :].rearrange("(b n) q -> n b q", b=2)
                        sp.dma_start(dst[P * m:P * (m + 1)], out[m % 2][part][:].bitcast(F32)
                                     .rearrange("p (b q) -> p b q", b=2)).then_inc(stored[m % 2], 16)

            load(0, 0)
            load(0, 1)
            store_q(0)
            load(0, 2)
            store_q(1)
            load(0, 3)
            store_k(0, 0)
            with sp.Fori(1, B) as b:
                load(b, 0)
                store_k(b - 1, 1)
                load(b, 1)
                store_k(b - 1, 2)
                load(b, 2)
                store_k(b - 1, 3)
                load(b, 3)
                store_k(b, 0)
            for r in range(1, 4):
                store_k(B - 1, r)
            sp.dma_start(k.wo_raw[:], k.wo.rearrange("(c p) n -> p c n", p=P)).then_inc(ffn_loaded, 16)
            sp.dma_start(k.g_raw[:], k.g.rearrange("(m p) d -> p m d", p=P)).then_inc(ffn_loaded, 16)
            sp.dma_start(k.u_raw[:], k.u.rearrange("(m p) d -> p m d", p=P)).then_inc(ffn_loaded, 16)
            sp.dma_start(k.d_raw[:], k.d.rearrange("(c p) f -> p c f", p=P)).then_inc(ffn_loaded, 16)
            for i in range(2):
                sp.wait_ge(stored[i], 32 * (QU // 2 + 2 * B))

        @block.gpsimd
        def _(pool):
            nc.gpsimd.memset(k.ident[:], 0.0).then_inc(id_zero, 1)
            pool.wait_ge(id_zero, 1)
            nc.gpsimd.affine_select(out=k.ident[:], in_=k.ident[:], compare_op=ALU.not_equal, fill=1.0, base=0,
                                    pattern=[[-1, P]], channel_multiplier=1).then_inc(id_ready, 1)
            for i, (lo, hi) in enumerate(((0, D), (D, D + P), (D + P, D + 2 * P))):
                pool.wait_ge(w_loaded[i], 16)
                nc.gpsimd.tensor_copy(w[0][:, :, lo:hi], wraw[:, :, lo:hi]).then_inc(w_hi_done, 1)
                pool.wait_ge(w_hi_done, i + 1)
                nc.gpsimd.tensor_tensor(w[1][:, :, lo:hi], wraw[:, :, lo:hi], w[0][:, :, lo:hi].bitcast(F32),
                                        ALU.subtract).then_inc(w_ready, 1)

        @block.tensor
        def _(pe):
            def turn(slot, tile0, n, np_):
                for j in range(n):
                    t = tile0 + j
                    if not (isinstance(t, int) and t < 4):
                        pe.wait_ge(turn_lo, t - 3)
                    for c in range(C):
                        mm = pe.transpose(turn_bank[j % 4][:, P * c:P * c + np_], tok[slot][0:np_, j, P * c:P * (c + 1)],
                                          k.ident[0:np_, 0:np_])
                    mm.then_inc(turned, 1)

            def turn_x(u):
                for j in range(4):
                    t = 4 * u + j
                    pe.wait_ge(ln_done, t + 1)
                    if t >= 4:
                        pe.wait_ge(turn_lo, t - 3)
                    for c in range(C):
                        mm = pe.transpose(turn_bank[j][:, P * c:P * (c + 1)], tok[u][:, j, P * c:P * (c + 1)], k.ident[:])
                    mm.then_inc(turned, 1)

            def turn_ctx(b, r):
                pe.wait_ge(tok_loaded[r % 2], 16 * (2 + 2 * b + r // 2))
                if r == 0:
                    pe.wait_ge(turn_lo, first_tile(b, 0))
                turn(r % 2, first_tile(b, r), tiles(r), rows(r))

            def q_of(u):
                pe.wait_ge(turn_lo, 4 * (u + 1))
                pe.wait_ge(w_ready, 1)
                for m in range(C):
                    n = 4 * u + m
                    if n >= 2:
                        pe.wait_ge(kq_lo, n - 1)
                    product(pe, kq_bank[n % 2], lambda p, c: w[p][:, c, P * m:P * (m + 1)],
                            lambda p, c: tokT[u][p][:, c, :], range(C)).then_inc(kq_ready, 1)

            def kv_of(b, r):
                n, np_ = tiles(r), rows(r)
                pe.wait_ge(turn_lo, first_tile(b, r) + n)
                pe.wait_ge(v_free, 4 * b + r + 1)
                for j in range(n):
                    mm = product(pe, v_bank[r % 2][0:np_, P * j:P * (j + 1)],
                                 lambda p, c: tokT[r % 2][p][:, c, P * j:P * j + np_],
                                 lambda p, c: w[p][:, c, D + P:D + 2 * P], range(C))
                mm.then_inc(v_ready, 1)
                cols = P * (n - 1) + np_ + np_ % 2
                pe.wait_ge(kq_lo, QU + 4 * b + r - 1)
                product(pe, kq_bank[r % 2][:, 0:cols], lambda p, c: w[p][:, c, D:D + P],
                        lambda p, c: tokT[r % 2][p][:, c, 0:cols], range(C)).then_inc(kq_ready, 1)

            pe.wait_ge(id_ready, 1)
            turn_x(0)
            turn_x(1)
            q_of(0)
            turn_ctx(0, 0)
            q_of(1)
            pe.wait_ge(w_ready, 3)
            with pe.Fori(0, B - 1) as b:
                for r in range(4):
                    turn_ctx(b + (r + 1) // 4, (r + 1) % 4)
                    kv_of(b, r)
            for r in range(4):
                if r < 3:
                    turn_ctx(B - 1, r + 1)
                kv_of(B - 1, r)

        @block.scalar
        def _(act):
            act.sem_inc(v_free, 2)

            def turn_part(slot, j, t, np_):
                act.wait_ge(turned, t + 1)
                src = turn_bank[j % 4].rearrange("p (c n) -> p c n", c=C)[:, :, 0:np_]
                nc.scalar.activation(tokT[slot][0][:, :, P * j:P * j + np_], src, ACT.Copy).then_inc(turn_hi, 1)

            def turn_x(u):
                for j in range(4):
                    turn_part(u, j, 4 * u + j, P)

            def turn_ctx(b, r):
                if isinstance(b, int) and b == 0 and r == 0:
                    act.wait_ge(kq_ready, 4)
                else:
                    act.wait_ge(kq_ready, QU + 4 * b + r - 1)
                for j in range(tiles(r)):
                    turn_part(r % 2, j, first_tile(b, r) + j, rows(r))

            def q_of(u):
                for m in range(C):
                    n = 4 * u + m
                    act.wait_ge(kq_ready, n + 1)
                    if n >= 2:
                        act.wait_ge(stored[n % 2], 32 * (n // 2))
                    nc.scalar.activation(out[n % 2][0][:], kq_bank[n % 2], ACT.Copy).then_inc(kq_hi, 1)

            def kv_of(b, r):
                n, np_ = tiles(r), rows(r)
                act.wait_ge(v_ready, 4 * b + r + 1)
                dst = k.v[0:np_, bass.ds(2 * b, 2), 4 * r:4 * r + n, :].rearrange("p h t d -> p t h d")
                src = v_bank[r % 2][0:np_, 0:P * n].rearrange("p (t h d) -> p t h d", t=n, h=2)
                nc.scalar.activation(dst, src, ACT.Copy).then_inc(v_free, 1)
                cols = P * (n - 1) + np_
                act.wait_ge(kq_ready, QU + 4 * b + r + 1)
                act.wait_ge(stored[r % 2], 32 * (QU // 2 + 2 * b + r // 2))
                nc.scalar.activation(out[r % 2][0][:, 0:cols], kq_bank[r % 2][:, 0:cols], ACT.Copy).then_inc(kq_hi, 1)

            act.wait_ge(eps_ready, 1)
            for u in range(2):
                act.wait_ge(var_ready, 4 * (u + 1))
                nc.scalar.activation(std[:, 4 * u:4 * u + 4], mean_var[:, 4 * u:4 * u + 4, 1], ACT.Sqrt,
                                     bias=k.eps[:]).then_inc(std_ready, 1)
            turn_x(0)
            turn_x(1)
            q_of(0)
            turn_ctx(0, 0)
            q_of(1)
            with act.Fori(0, B - 1) as b:
                for r in range(4):
                    turn_ctx(b + (r + 1) // 4, (r + 1) % 4)
                    kv_of(b, r)
            for r in range(4):
                if r < 3:
                    turn_ctx(B - 1, r + 1)
                kv_of(B - 1, r)

        @block.vector
        def _(dve):
            def turn_part(slot, j, t, np_):
                dve.wait_ge(turn_hi, t + 1)
                src = turn_bank[j % 4].rearrange("p (c n) -> p c n", c=C)[:, :, 0:np_]
                hi, lo = (tokT[slot][p][:, :, P * j:P * j + np_] for p in range(2))
                nc.vector.tensor_tensor(lo, src, hi.bitcast(F32), ALU.subtract).then_inc(turn_lo, 1)

            def turn_ctx(b, r):
                for j in range(tiles(r)):
                    turn_part(r % 2, j, first_tile(b, r) + j, rows(r))

            def kq_part(n, slot, cols):
                dve.wait_ge(kq_hi, n + 1)
                nc.vector.tensor_tensor(out[slot][1][:, 0:cols], kq_bank[slot][:, 0:cols],
                                        out[slot][0][:, 0:cols].bitcast(F32), ALU.subtract).then_inc(kq_lo, 1)

            def q_of(u):
                for m in range(C):
                    kq_part(4 * u + m, m % 2, 4 * P)

            def kv_of(b, r):
                kq_part(QU + 4 * b + r, r % 2, P * (tiles(r) - 1) + rows(r))

            nc.vector.memset(k.eps[:], EPS).then_inc(eps_ready, 1)
            for u in range(2):
                dve.wait_ge(tok_loaded[u], 16)
                for j in range(4):
                    nc.vector.bn_stats(stats[:, 4 * u + j, :], tok[u][:, j, :]).then_inc(stats_ready, 1)
                dve.wait_ge(stats_ready, 4 * (u + 1))
                for j in range(4):
                    nc.vector.bn_aggr(mean_var[:, 4 * u + j, :], stats[:, 4 * u + j, :]).then_inc(var_ready, 1)
                dve.wait_ge(std_ready, u + 1)
                nc.vector.reciprocal(rstd[:, 4 * u:4 * u + 4], std[:, 4 * u:4 * u + 4]).then_inc(rstd_ready, 1)
                dve.wait_ge(rstd_ready, u + 1)
                for j in range(4):
                    nc.vector.tensor_scalar(tok[u][:, j, :], tok[u][:, j, :], mean_var[:, 4 * u + j, 0:1],
                                            rstd[:, 4 * u + j:4 * u + j + 1], ALU.subtract, ALU.mult
                                            ).then_inc(ln_done, 1)
            for u in range(2):
                for j in range(4):
                    turn_part(u, j, 4 * u + j, P)
            q_of(0)
            turn_ctx(0, 0)
            q_of(1)
            with dve.Fori(0, B - 1) as b:
                for r in range(4):
                    turn_ctx(b + (r + 1) // 4, (r + 1) % 4)
                    kv_of(b, r)
            for r in range(4):
                if r < 3:
                    turn_ctx(B - 1, r + 1)
                kv_of(B - 1, r)


def attend(nc, k):
    with ExitStack() as ctx:
        base = [k_base(nc) + AT_WORK]

        def sb(name, shape, dt):
            size = 4
            for n in shape[1:]:
                size *= n
            t = nc.alloc_sbuf_tensor_at(name, shape, dt, offset=base[0])
            base[0] += (size + 63) // 64 * 64
            return t

        def sem(name):
            return ctx.enter_context(nc.semaphore(name))

        ks = [sb(f"ks{i}", [P, SK], F32R) for i in range(FOUR)]
        qs = [sb(f"qs{i}", [P, QC], F32R) for i in range(FOUR)]
        vg = [sb(f"vg{i}", [P, TILES, 2 * HD], F32) for i in range(2)]
        probs = [sb(f"probs{i}", [P, QC], F32) for i in range(FOUR)]
        pv = [sb(f"pv{i}", [P, S], F32) for i in range(2)]
        piece_max = [sb(f"piece_max{i}", [P, UNITS], F32) for i in range(2)]
        neg_max = [sb(f"neg_max{i}", [P, NQ], F32) for i in range(2)]
        max_hi = [sb(f"max_hi{i}", [NQ, P], F32R) for i in range(2)]
        max_lo = [sb(f"max_lo{i}", [NQ, P], F32R) for i in range(2)]
        score_bank = [k.bank[:, 2 * i:2 * i + 2, :].rearrange("p b n -> p (b n)") for i in range(2)]
        pv_bank = k.bank[:, 4, 0:S]
        row_bank = [k.bank[:, 5 + i, :] for i in range(3)]

        fixed_rows = sem("fixed_rows")
        loaded = [sem(f"qk_loaded{i}") for i in range(FOUR)]
        max_loaded = [sem(f"max_loaded{i}") for i in range(FOUR)]
        rows_ready = sem("rows_ready")
        rows_free = sem("rows_free")
        max_ready = sem("max_ready")
        max_split = sem("max_split")
        scores_ready = sem("scores_ready")
        probs_ready = sem("probs_ready")
        v_ready = sem("vg_ready")
        pv_done = sem("pv_done")
        pv_free = sem("pv_free")
        pv_stored = [sem(f"pv_stored{i}") for i in range(2)]

        TURNS = GROUPS // FOUR
        AHEAD = TILES + 6
        PER_TURN = FOUR * (UNITS + 1)

        def keys(t):
            return P if t < TILES - 1 else LAST

        def units(part):
            return range(UNITS * part // TILES, UNITS * (part + 1) // TILES)

        def row_steps(g, i, t, last):
            ahead, part = divmod(t + AHEAD - TILES, TILES)
            g, i = g + 1 + ahead, i + 1 + ahead
            steps = []
            for u in units(part):
                if u == 3 and not (last and i > FOUR):
                    steps.append((g - 1, i - 1, "max"))
                if not (last and i >= FOUR):
                    steps.append((g, i, u))
            return steps

        def index(g, step, last=False):
            if step == "max":
                return (UNITS + 1) * (g + 1) + (2 if not last else -1)
            if isinstance(g, int) and g == 0:
                return step
            return (UNITS + 1) * g - 1 + step + (step >= 3)

        def bank_of(g, step):
            return row_bank[index(0 if step == "max" or (isinstance(g, int) and g == 0) else 3, step) % 3]

        def first_rows(do):
            for u in range(UNITS):
                do(0, 0, u)
            for part in range(AHEAD - TILES):
                for u in units(part):
                    if u == 3:
                        do(0, 0, "max")
                    do(1, 1, u)

        def turn_slots(last):
            return [divmod(s, TILES) for s in range(1, FOUR * TILES + (0 if last else 1))]

        block = ctx.enter_context(nc.Block())

        @block.gpsimd
        def _(pool):
            for i in range(FOUR):
                nc.gpsimd.memset(ks[i][ZROW:MROW, :].bitcast(F32), 0.0).then_inc(fixed_rows, 1)
                nc.gpsimd.memset(ks[i][MROW:SROWS, :].bitcast(F32), 1.0).then_inc(fixed_rows, 1)
                nc.gpsimd.memset(qs[i][ZROW:MROW, :].bitcast(F32), 0.0).then_inc(fixed_rows, 1)
            pool.wait_ge(fixed_rows, 3 * FOUR)
            for i in range(2):
                nc.gpsimd.memset(vg[i][:, :, HD:], 1.0).then_inc(fixed_rows, 1)

            def copy(h, i):
                for rows, t0, t1 in ((P, 0, TILES - 1), (LAST, TILES - 1, TILES)):
                    src = k.v[0:rows, bass.ds(h + i // FOUR, 1), t0:t1, HD * (i % FOUR):HD * (i % FOUR + 1)]
                    nc.gpsimd.tensor_copy(vg[i % 2][0:rows, t0:t1, 0:HD],
                                          src.rearrange("p o t d -> p (o t) d")).then_inc(v_ready, 1)

            copy(0, 0)
            copy(0, 1)
            with pool.Fori(0, TURNS - 1) as h:
                for i in range(FOUR):
                    pool.wait_ge(pv_done, TILES * (FOUR * h + i + 1))
                    copy(h, i + 2)
            for i in range(FOUR - 2):
                pool.wait_ge(pv_done, TILES * (GROUPS - FOUR + i + 1))
                copy(TURNS - 1, i + 2)

        @block.sync
        def _(sp):
            def load(h, i):
                g = FOUR * h + i
                for part in range(2):
                    sp.dma_start(ks[i][2 * HD * part:2 * HD * (part + 1), :].bitcast(F32),
                                 k.k_dram[part, bass.ds(HD * g, HD), :].partition_broadcast(2)
                                 ).then_inc(loaded[i], 16)
                    src = k.q_dram[part, bass.ds(REP * HD * g, REP * HD), :].rearrange("(h d) q -> d h q", h=REP)
                    for row in (HD * part, HD * (part + 2)):
                        sp.dma_start(qs[i][row:row + HD, :].bitcast(F32).rearrange("d (h q) -> d h q", h=REP),
                                     src).then_inc(loaded[i], 16)

            def put_max(g, i, last=False):
                sp.wait_ge(rows_free, index(g, "max", last) + 1 + 3)
                for n, src in enumerate((max_hi, max_lo)):
                    row = MROW + n
                    sp.dma_start(qs[i % FOUR][row:row + 1, :].bitcast(F32).rearrange("o (j q) -> o j q", j=NQ),
                                 src[i % 2][:].bitcast(F32)).then_inc(max_loaded[i % FOUR], 16)

            def put_pv(h, i):
                g = FOUR * h + i
                sp.wait_ge(pv_free, g + 2)
                sp.dma_start(k.pv_dram[bass.ds(P * g, P), :], pv[i % 2][:]).then_inc(pv_stored[i % 2], 16)

            for i in range(FOUR):
                load(0, i)
            put_max(0, 0)
            with sp.Fori(0, TURNS - 1) as h:
                for i in range(FOUR):
                    put_max(FOUR * h + i + 1, i + 1)
                    sp.wait_ge(scores_ready, TILES * (FOUR * h + i + 1))
                    load(h + 1, i)
                    put_pv(h, i)
            for i in range(FOUR):
                if i < FOUR - 1:
                    put_max(GROUPS - FOUR + i + 1, i + 1, last=i == FOUR - 2)
                put_pv(TURNS - 1, i)
            for i in range(2):
                sp.wait_ge(pv_stored[i], 16 * (GROUPS // 2 + 1))

        @block.tensor
        def _(pe):
            def rows_step(g, i, step, last=False):
                bank = bank_of(g, step)
                if step == "max":
                    pe.wait_ge(max_ready, g + 1)
                pe.wait_ge(rows_free, index(g, step, last) + 1)
                if step == "max":
                    pe.transpose(bank[0:NQ, 0:P], neg_max[i % 2][:], k.ident[:]).then_inc(rows_ready, 1)
                    return
                if step == 0:
                    pe.wait_ge(loaded[i % FOUR], 24 * (g - i % FOUR) + 96)
                j, piece = divmod(step, PIECES)
                pe.matmul(bank[:, 0:PIECE], qs[i % FOUR][0:MROW, P * j:P * (j + 1)],
                          ks[i % FOUR][0:MROW, STARTS[piece]:STARTS[piece] + PIECE],
                          start=True, stop=True).then_inc(rows_ready, 1)

            def scores(h, i, t):
                if t == 0:
                    pe.wait_ge(max_loaded[i % FOUR], 32 * (h + i // FOUR + 1))
                s = TILES * i + t
                for half in range(2):
                    mm = pe.matmul(score_bank[s % 2][0:keys(t), 512 * half:512 * (half + 1)],
                                   ks[i % FOUR][0:SROWS, P * t:P * t + keys(t)],
                                   qs[i % FOUR][0:SROWS, 512 * half:512 * (half + 1)], start=True, stop=True)
                mm.then_inc(scores_ready, 1)

            def p_v(h, i, t):
                g, s = FOUR * h + i, TILES * i + t
                pe.wait_ge(probs_ready, TILES * g + t + 1)
                if t == 0:
                    pe.wait_ge(v_ready, 2 * (g + 1))
                    pe.wait_ge(pv_free, g + 1)
                for j in range(REP):
                    mm = pe.matmul(pv_bank[32 * j:32 * (j + 1), :], vg[i % 2][0:keys(t), t, :],
                                   probs[s % FOUR][0:keys(t), S * j:S * (j + 1)],
                                   start=t == 0, stop=t == TILES - 1)
                mm.then_inc(pv_done, 1)

            def slot(h, i, t, last):
                scores(h, i, t)
                for g, ii, step in row_steps(FOUR * h + i, i, t, last):
                    rows_step(g, ii, step, last and ii == FOUR - 1)
                p_v(h, *divmod(TILES * i + t - 1, TILES))

            pe.wait_ge(fixed_rows, 3 * FOUR + 2)
            first_rows(rows_step)
            scores(0, 0, 0)
            for g, ii, step in row_steps(0, 0, 0, False):
                rows_step(g, ii, step)
            with pe.Fori(0, TURNS - 1) as h:
                for i, t in turn_slots(False):
                    slot(h, i, t, False)
            for i, t in turn_slots(True):
                slot(TURNS - 1, i, t, True)
            p_v(TURNS - 1, FOUR - 1, TILES - 1)

        @block.scalar
        def _(act):
            act.sem_inc(pv_free, 1)
            for i in range(2):
                act.sem_inc(pv_stored[i], 16)

            def exponential(h, i, t):
                s = TILES * i + t
                act.wait_ge(scores_ready, TILES * FOUR * h + s + 1)
                nc.scalar.activation(probs[s % FOUR][0:keys(t), :], score_bank[s % 2][0:keys(t), :], ACT.Exp,
                                     scale=HD ** -0.5).then_inc(probs_ready, 1)

            def take_pv(h, i):
                g = FOUR * h + i
                act.wait_ge(pv_done, TILES * (g + 1))
                act.wait_ge(pv_stored[i % 2], 16 * (2 * h + i // 2 + 1))
                nc.scalar.activation(pv[i % 2][:], pv_bank, ACT.Copy).then_inc(pv_free, 1)

            exponential(0, 0, 0)
            with act.Fori(0, TURNS - 1) as h:
                for i, t in turn_slots(False):
                    exponential(h, i, t)
                    if t == 0:
                        take_pv(h, i - 1)
            for i, t in turn_slots(True):
                exponential(TURNS - 1, i, t)
                if t == 0:
                    take_pv(TURNS - 1, i - 1)
            take_pv(TURNS - 1, FOUR - 1)

        @block.vector
        def _(dve):
            dve.sem_inc(rows_free, 3)

            def rows_step(g, i, step, last=False):
                bank, n = bank_of(g, step), index(g, step, last)
                dve.wait_ge(rows_ready, n + 1)
                if step == "max":
                    nc.vector.tensor_copy(max_hi[i % 2][:], bank[0:NQ, 0:P]).then_inc(max_split, 1)
                    dve.wait_ge(max_split, g + 1)
                    nc.vector.tensor_tensor(max_lo[i % 2][:], bank[0:NQ, 0:P], max_hi[i % 2][:].bitcast(F32),
                                            ALU.subtract).then_inc(rows_free, 1)
                    return
                nc.vector.tensor_reduce(piece_max[i % 2][:, step:step + 1], bank[:, 0:PIECE], AX.X, ALU.max
                                        ).then_inc(rows_free, 1)
                if step == UNITS - 1:
                    dve.wait_ge(rows_free, n + 1 + 3)
                    nc.vector.tensor_reduce(neg_max[i % 2][:], piece_max[i % 2][:].rearrange("p (j c) -> p j c", c=PIECES),
                                            AX.X, ALU.max, negate=True).then_inc(max_ready, 1)

            first_rows(rows_step)
            for g, ii, step in row_steps(0, 0, 0, False):
                rows_step(g, ii, step)
            with dve.Fori(0, TURNS - 1) as h:
                for i, t in turn_slots(False):
                    for g, ii, step in row_steps(FOUR * h + i, i, t, False):
                        rows_step(g, ii, step)
            for i, t in turn_slots(True):
                for g, ii, step in row_steps(FOUR * (TURNS - 1) + i, i, t, True):
                    rows_step(g, ii, step, ii == FOUR - 1)


def prepare(nc, k):
    with ExitStack() as ctx:
        def sem(name):
            return ctx.enter_context(nc.semaphore(name))

        gate_raw = k.at("gate_raw", [E, D], AT_WORK3)
        bank = [k.bank[:, i, :] for i in range(4)]
        N = 3 * FC + 1

        gate_loaded = sem("gate_loaded")
        turned = sem("w_turned")
        hi_done = sem("w_turn_hi")
        lo_done = sem("w_turn_lo")
        wo_hi = sem("wo_hi")
        pool_done = sem("pool_prepared")

        def blocks(n):
            m = n % FC
            if n < FC:
                return [k.g_raw[:, m, P * c:P * (c + 1)] for c in range(C)]
            if n < 2 * FC:
                return [k.u_raw[:, m, P * c:P * (c + 1)] for c in range(C)]
            if n < 3 * FC:
                return [k.d_raw[:, c, P * m:P * (m + 1)] for c in range(C)]
            return [gate_raw[:, P * c:P * (c + 1)] for c in range(C)]

        def home(n, p):
            m = n % FC
            if n < 2 * FC:
                return (k.gT, k.uT)[n // FC][p][:, :, P * m:P * (m + 1)]
            if n < 3 * FC:
                return k.dT[p][:, m, :].rearrange("p (c n) -> p c n", c=C)
            return k.gateT[p][:, :, 0:E]

        def width(n):
            return P if n < 3 * FC else E

        def turned_view(n):
            return bank[n % 4][:, 0:C * width(n)].rearrange("p (c n) -> p c n", c=C)

        block = ctx.enter_context(nc.Block())

        @block.sync
        def _(sp):
            sp.dma_start(gate_raw[:], k.gate_w).then_inc(gate_loaded, 16)
            sp.dma_start(k.res[:], k.x.rearrange("b (t p) d -> p (b t) d", p=P)).then_inc(k.x_loaded, 16)
            sp.wait_ge(gate_loaded, 16)

        @block.gpsimd
        def _(pool):
            pool.wait_ge(k.ffn_loaded, 64)
            nc.gpsimd.tensor_copy(k.wo_part[0][:], k.wo_raw[:]).then_inc(wo_hi, 1)
            pool.wait_ge(wo_hi, 1)
            nc.gpsimd.tensor_tensor(k.wo_part[1][:], k.wo_raw[:], k.wo_part[0][:].bitcast(F32), ALU.subtract
                                    ).then_inc(pool_done, 1)

        @block.tensor
        def _(pe):
            pe.wait_ge(k.ffn_loaded, 64)
            pe.wait_ge(gate_loaded, 16)
            for n in range(N):
                if n >= 4:
                    pe.wait_ge(lo_done, n - 3)
                for c, blk in enumerate(blocks(n)):
                    w = width(n)
                    mm = pe.transpose(bank[n % 4][:, w * c:w * (c + 1)], blk, k.ident[0:w, 0:w])
                mm.then_inc(turned, 1)

        @block.scalar
        def _(act):
            for n in range(N):
                act.wait_ge(turned, n + 1)
                nc.scalar.activation(home(n, 0), turned_view(n), ACT.Copy).then_inc(hi_done, 1)

        @block.vector
        def _(dve):
            for p in range(2):
                nc.vector.memset(k.gateT[p][:, :, E:].bitcast(F32), 0.0)
            for n in range(N):
                dve.wait_ge(hi_done, n + 1)
                nc.vector.tensor_tensor(home(n, 1), turned_view(n), home(n, 0).bitcast(F32), ALU.subtract
                                        ).then_inc(lo_done, 1)


def mix(nc, k):
    with ExitStack() as ctx:
        def sem(name):
            return ctx.enter_context(nc.semaphore(name))

        T = S // P
        NT = B * T
        room = {"small": AT_WORK3 + 20 * KB, "early": AT_WORK3}

        def tiny(name, shape, dt=F32, where="small"):
            size = 4
            for n in shape[1:]:
                size *= n
            t = k.at(name, shape, room[where], dt)
            room[where] += (size + 63) // 64 * 64
            return t

        num = k.at("num", [P, C, S], AT_WORK3)
        den = k.at("den", [P, C, S], AT_WORK3 + 4 * KB)
        at = [k.at(f"att_{n}", [P, C, S], AT_WORK3 + (8 + 4 * i) * KB, F32R) for i, n in enumerate(("hi", "lo"))]
        xn = [k.at(f"xn{t}", [P, D], AT_WORK3 + (16 + 2 * t) * KB) for t in range(2)]
        stats, mean_var = tiny("stats3", [P, NT, 6]), tiny("mean_var3", [P, NT, 2])
        std, rstd = tiny("std3", [P, NT]), tiny("rstd3", [P, NT])
        logits, top_logit = tiny("logits", [P, NT, E]), tiny("top_logit", [P, NT, 8])
        exps, total, inv_total = tiny("exps", [P, NT, E]), tiny("total", [P, NT]), tiny("inv_total", [P, NT])
        prob, top, top_at = tiny("prob", [P, NT, E]), tiny("top", [P, NT, 8]), tiny("top_at", [P, NT, 8], U32)
        two, inv_two = tiny("two", [P, NT]), tiny("inv_two", [P, NT])
        share, at_f = tiny("share", [P, NT, 2]), tiny("at_f", [P, NT, 2])
        expert_no = tiny("expert_no", [P, E])
        ltT = tiny("ltT", [E, B * S], where="early")
        w1, w2, w = (tiny(f"w_{n}", [P, NT, E], where="early") for n in ("first", "second", "both"))
        wparts = tiny("wparts", [P, NT, 2 * E], where="early")

        wo_bank = [k.bank[:, i, :] for i in range(T)]
        turn_bank = [k.bank[:, 2 + i, :] for i in range(2)]
        lt_bank = [k.bank[:, 4 + i, 0:S] for i in range(2)]
        logit_bank = k.bank[:, 0, 0:NT * E]
        wt_bank = k.bank[:, 6:8, :].rearrange("p b n -> p (b n)")

        loaded = sem("att_loaded")
        inv_ready = sem("inv_ready")
        att_ready = sem("att_ready")
        att_hi, att_lo = sem("att_hi"), sem("att_lo")
        wo_ready = sem("wo_ready")
        wo_free = sem("wo_free")
        stats_ready = sem("stats3_ready")
        var_ready = sem("var3_ready")
        std_ready = sem("std3_ready")
        rstd_ready = sem("rstd3_ready")
        xn_ready = sem("xn_ready")
        turned = sem("xn_turned")
        turn_hi, turn_lo = sem("xn_hi"), sem("xn_lo")
        lt_ready, lt_copied = sem("lt_ready"), sem("lt_copied")
        logit_turned, logit_ready = sem("logit_turned"), sem("logit_ready")
        less_top = sem("less_top")
        exp_ready = sem("exp_ready")
        step = sem("router_step")
        w_split = sem("w_split")
        wt_turned, wt_ready = sem("wt_turned"), sem("wt_ready")
        consts = sem("mix_consts")

        block = ctx.enter_context(nc.Block())

        @block.sync
        def _(sp):
            with sp.Fori(0, B) as b:
                sp.wait_ge(k.att_free, b + 1)
                for c in range(C):
                    for half, dst in enumerate((num, den)):
                        rows = k.pv_dram[bass.ds(KV * P * b + 2 * P * c, 2 * P), :]
                        src = rows.rearrange("(j n d) q -> n j d q", j=8, n=2)[half]
                        sp.dma_start(dst[:, c, :], src).then_inc(loaded, 16)

        @block.gpsimd
        def _(pool):
            nc.gpsimd.memset(k.expand[:].bitcast(F32), 0.0).then_inc(consts, 1)
            nc.gpsimd.memset(k.wT[:].bitcast(F32), 0.0).then_inc(consts, 1)
            nc.gpsimd.iota(expert_no[:], [[1, E]], base=0, channel_multiplier=0,
                           allow_small_or_imprecise_dtypes=True).then_inc(consts, 1)
            nc.gpsimd.memset(k.band[0][:], 1.0).then_inc(consts, 1)
            nc.gpsimd.memset(k.band[1][:], 1.0).then_inc(consts, 1)
            pool.wait_ge(consts, 5)
            for i in range(2):
                nc.gpsimd.affine_select(out=k.band[i][:], in_=k.band[i][:], compare_op=ALU.is_ge, fill=0.0,
                                        base=INTER * E * i, pattern=[[1, F]], channel_multiplier=-INTER
                                        ).then_inc(consts, 1)
                pool.wait_ge(consts, 6 + 2 * i)
                nc.gpsimd.affine_select(out=k.band[i][:], in_=k.band[i][:], compare_op=ALU.is_ge, fill=0.0,
                                        base=INTER - 1 - INTER * E * i, pattern=[[-1, F]], channel_multiplier=INTER
                                        ).then_inc(consts, 1)
                pool.wait_ge(consts, 7 + 2 * i)
            nc.gpsimd.tensor_tensor(k.expand[0:2 * E, :], k.band[0][:], k.band[1][:], ALU.add).then_inc(consts, 1)

        @block.tensor
        def _(pe):
            with pe.Fori(0, B) as b:
                pe.wait_ge(att_lo, b + 1)
                for t in range(T):
                    pe.wait_ge(wo_free, T * b + t + 1)
                    product(pe, wo_bank[t], lambda p, c: at[p][:, c, P * t:P * (t + 1)],
                            lambda p, c: k.wo_part[p][:, c, :], range(C)).then_inc(wo_ready, 1)
            for b in range(B):
                for t in range(T * b, T * (b + 1)):
                    pe.wait_ge(xn_ready, t + 1)
                    if t >= 2:
                        pe.wait_ge(turn_lo, t - 1)
                    for c in range(C):
                        mm = pe.transpose(turn_bank[t % 2][:, P * c:P * (c + 1)], xn[t % 2][:, P * c:P * (c + 1)],
                                          k.ident[:])
                    mm.then_inc(turned, 1)
                pe.wait_ge(turn_lo, T * (b + 1))
                if b >= 2:
                    pe.wait_ge(lt_copied, b - 1)
                product(pe, lt_bank[b % 2], lambda p, c: k.gateT[p][:, c, :],
                        lambda p, c: k.xnT[p][:, c, S * b:S * (b + 1)], range(C)).then_inc(lt_ready, 1)
            for b in range(B):
                pe.wait_ge(lt_copied, b + 1)
                for t in range(T * b, T * (b + 1)):
                    mm = pe.transpose(logit_bank[:, E * t:E * (t + 1)], ltT[:, P * t:P * (t + 1)], k.ident[0:E, 0:E])
            mm.then_inc(logit_turned, 1)
            pe.wait_ge(w_split, 1)
            for t in range(NT):
                mm = pe.transpose(wt_bank[0:2 * E, P * t:P * (t + 1)], wparts[:, t, :], k.ident[:])
            mm.then_inc(wt_turned, 1)

        @block.scalar
        def _(act):
            act.wait_ge(consts, 3)
            with act.Fori(0, B) as b:
                act.wait_ge(att_ready, b + 1)
                act.wait_ge(wo_free, T * (b + 1))
                nc.scalar.activation(at[0][:], num[:], ACT.Copy).then_inc(att_hi, 1)
            act.wait_ge(var_ready, NT)
            nc.scalar.activation(std[:], mean_var[:, :, 1], ACT.Sqrt, bias=k.eps[:]).then_inc(std_ready, 1)
            for b in range(B):
                for t in range(T * b, T * (b + 1)):
                    act.wait_ge(turned, t + 1)
                    nc.scalar.activation(k.xnT[0][:, :, P * t:P * (t + 1)],
                                         turn_bank[t % 2].rearrange("p (c n) -> p c n", c=C), ACT.Copy
                                         ).then_inc(turn_hi, 1)
                act.wait_ge(lt_ready, b + 1)
                nc.scalar.activation(ltT[:, S * b:S * (b + 1)], lt_bank[b % 2][0:E, :], ACT.Copy).then_inc(lt_copied, 1)
            act.wait_ge(logit_turned, 1)
            nc.scalar.activation(logits[:].rearrange("p t e -> p (t e)"), logit_bank, ACT.Copy).then_inc(logit_ready, 1)
            act.wait_ge(less_top, 1)
            nc.scalar.activation(exps[:], logits[:], ACT.Exp).then_inc(exp_ready, 1)
            act.wait_ge(wt_turned, 1)
            nc.scalar.activation(k.wT[0:2 * E, :], wt_bank[0:2 * E, :], ACT.Copy).then_inc(wt_ready, 1)
            act.wait_ge(wt_ready, 1)

        @block.vector
        def _(dve):
            dve.sem_inc(wo_free, T)
            dve.sem_inc(k.att_free, 1)
            dve.wait_ge(k.x_loaded, 16)
            V = nc.vector
            with dve.Fori(0, B) as b:
                dve.wait_ge(loaded, 16 * 2 * C * (b + 1))
                V.reciprocal(den[:], den[:]).then_inc(inv_ready, 1)
                dve.wait_ge(inv_ready, b + 1)
                V.tensor_tensor(num[:], num[:], den[:], ALU.mult).then_inc(att_ready, 1)
                dve.wait_ge(att_hi, b + 1)
                V.tensor_tensor(at[1][:], num[:], at[0][:].bitcast(F32), ALU.subtract).then_inc(att_lo, 1)
                dve.wait_ge(att_lo, b + 1)
                dve.sem_inc(k.att_free, 1)
                for t in range(T):
                    res = k.res[:, bass.ds(T * b + t, 1), :].rearrange("p o d -> p (o d)")
                    dve.wait_ge(wo_ready, T * b + t + 1)
                    V.tensor_tensor(res, wo_bank[t], res, ALU.add).then_inc(wo_free, 1)
            dve.wait_ge(wo_free, T * (B + 1))
            for t in range(NT):
                V.bn_stats(stats[:, t, :], k.res[:, t, :]).then_inc(stats_ready, 1)
            dve.wait_ge(stats_ready, NT)
            for t in range(NT):
                V.bn_aggr(mean_var[:, t, :], stats[:, t, :]).then_inc(var_ready, 1)
            dve.wait_ge(std_ready, 1)
            V.reciprocal(rstd[:], std[:]).then_inc(rstd_ready, 1)
            dve.wait_ge(rstd_ready, 1)

            def split(t):
                dve.wait_ge(turn_hi, t + 1)
                hi, lo = (k.xnT[p][:, :, P * t:P * (t + 1)] for p in range(2))
                V.tensor_tensor(lo, turn_bank[t % 2].rearrange("p (c n) -> p c n", c=C), hi.bitcast(F32),
                                ALU.subtract).then_inc(turn_lo, 1)

            for t in range(NT):
                if t >= 2:
                    dve.wait_ge(turned, t - 1)
                V.tensor_scalar(xn[t % 2][:], k.res[:, t, :], mean_var[:, t, 0:1], rstd[:, t:t + 1], ALU.subtract,
                                ALU.mult).then_inc(xn_ready, 1)
                if t >= 1:
                    split(t - 1)
            split(NT - 1)
            done = [0]

            def mark(ins):
                done[0] += 1
                ins.then_inc(step, 1)

            def marked():
                dve.wait_ge(step, done[0])

            def over(column):
                return column.broadcast_to([P, NT, E])

            dve.wait_ge(logit_ready, 1)
            dve.wait_ge(consts, 3)
            for t in range(NT):
                mark(V.max(top_logit[:, t, :], logits[:, t, :]))
            marked()
            V.tensor_tensor(logits[:], logits[:], over(top_logit[:, :, 0:1]), ALU.subtract).then_inc(less_top, 1)
            dve.wait_ge(exp_ready, 1)
            mark(V.tensor_reduce(total[:], exps[:], AX.X, ALU.add))
            marked()
            mark(V.reciprocal(inv_total[:], total[:]))
            marked()
            mark(V.tensor_tensor(prob[:], exps[:], over(inv_total[:].unsqueeze(2)), ALU.mult))
            marked()
            for t in range(NT):
                mark(V.max(top[:, t, :], prob[:, t, :]))
            marked()
            for t in range(NT):
                mark(V.max_index(top_at[:, t, :], top[:, t, :], prob[:, t, :]))
            mark(V.tensor_tensor(two[:], top[:, :, 0], top[:, :, 1], ALU.add))
            marked()
            mark(V.reciprocal(inv_two[:], two[:]))
            mark(V.tensor_copy(at_f[:], top_at[:, :, 0:2]))
            marked()
            mark(V.tensor_tensor(share[:], top[:, :, 0:2], inv_two[:].unsqueeze(2).broadcast_to([P, NT, 2]), ALU.mult))
            numbers = expert_no[:].unsqueeze(1).broadcast_to([P, NT, E])
            for dst, n in ((w1, 0), (w2, 1)):
                mark(V.tensor_tensor(dst[:], numbers, over(at_f[:, :, n:n + 1]), ALU.is_equal))
            marked()
            for dst, n in ((w1, 0), (w2, 1)):
                mark(V.tensor_tensor(dst[:], dst[:], over(share[:, :, n:n + 1]), ALU.mult))
            marked()
            mark(V.tensor_tensor(w[:], w1[:], w2[:], ALU.add))
            marked()
            mark(V.tensor_copy(wparts[:, :, 0:E].bitcast(F32R), w[:]))
            marked()
            V.tensor_tensor(wparts[:, :, E:], w[:], wparts[:, :, 0:E], ALU.subtract).then_inc(w_split, 1)


def experts(nc, k):
    with ExitStack() as ctx:
        def sem(name):
            return ctx.enter_context(nc.semaphore(name))

        T = S // P
        h = [k.at(f"h_{n}", [P, FC, S], AT_WORK3 + 7 * KB * i, F32R) for i, n in enumerate(("hi", "lo"))]
        work = AT_WORK3 + 14 * KB
        BANK = (0, 1, 0, 1, 0, 1, 2)
        sig = [k.at(f"sig{i}", [P, S], work + KB * (7 + i)) for i in range(3)]
        act_ = k.at("gated", [P, S], work + 2 * KB)
        up_ = k.at("gated_up", [P, S], work + 3 * KB)
        full = k.at("h_full", [P, S], work + 4 * KB)
        one = k.at("one_plus", [P, S], work + 5 * KB)
        inv = k.at("inv_plus", [P, S], work + 6 * KB)
        gu_bank = [k.bank[:, i, :] for i in range(3)]
        share_bank = [k.bank[:, 3 + i, 0:S] for i in range(3)]
        down_bank = [k.bank[:, 6 + t, :] for t in range(T)]

        gu_ready = sem("gu_ready")
        exp_ready = sem("ffn_exp_ready")
        step = sem("ffn_step")
        h_ready = sem("h_ready")
        down_ready = sem("down_ready")
        down_free = sem("down_free")
        y_ready = sem("y_ready")
        stored = sem("y_stored")

        def turn_slots(last):
            return [divmod(s, FC) for s in range(2, FC + 2)]

        block = ctx.enter_context(nc.Block())

        @block.sync
        def _(sp):
            y = k.y.rearrange("b (t p) d -> p b t d", p=P)
            with sp.Fori(0, B) as b:
                sp.wait_ge(y_ready, T * (b + 1))
                sp.dma_start(y[:, bass.ds(b, 1)].rearrange("p o t d -> p (o t) d"),
                             k.res[:, bass.ds(T * b, T), :]).then_inc(stored, 16)
            sp.wait_ge(stored, 16 * B)

        @block.tensor
        def _(pe):
            def first(b, m):
                n = FC * b + m
                if not isinstance(n, int) or n >= 2:
                    pe.wait_ge(h_ready, n - 1)
                for i, w in enumerate((k.gT, k.uT)):
                    product(pe, gu_bank[BANK[m]][:, S * i:S * (i + 1)], lambda p, c: w[p][:, c, P * m:P * (m + 1)],
                            lambda p, c: k.xnT[p][:, c, bass.ds(S * b, S)], range(C))
                pe.matmul(share_bank[BANK[m]], k.expand[:, P * m:P * (m + 1)], k.wT[:, bass.ds(S * b, S)],
                          start=True, stop=True).then_inc(gu_ready, 1)

            def second(b, m):
                pe.wait_ge(h_ready, FC * b + m + 1)
                if m == 0:
                    pe.wait_ge(down_free, b + 1)
                for t in range(T):
                    mm = product(pe, down_bank[t], lambda p, c: h[p][:, c, P * t:P * (t + 1)],
                                 lambda p, c: k.dT[p][:, c, :], [m], first=m == 0, last=m == FC - 1)
                if m == FC - 1:
                    mm.then_inc(down_ready, 1)

            first(0, 0)
            first(0, 1)
            with pe.Fori(0, B - 1) as b:
                for i, m in turn_slots(False):
                    first(b + i, m)
                    second(b, (FC * i + m) - 2)
            for i, m in turn_slots(True):
                if i == 0:
                    first(B - 1, m)
                second(B - 1, FC * i + m - 2)

        @block.scalar
        def _(act):
            with act.Fori(0, B) as b:
                for m in range(FC):
                    act.wait_ge(gu_ready, FC * b + m + 1)
                    nc.scalar.activation(sig[BANK[m]][:], gu_bank[BANK[m]][:, 0:S], ACT.Exp, scale=-1.0
                                         ).then_inc(exp_ready, 1)

        @block.vector
        def _(dve):
            dve.sem_inc(down_free, 1)
            V = nc.vector
            STEPS = 6

            def gate(b, m):
                n = FC * b + m
                bank = BANK[m]
                dve.wait_ge(exp_ready, n + 1)
                ops = [lambda: V.tensor_scalar(one[:], sig[BANK[m]][:], 1.0, None, ALU.add),
                       lambda: V.reciprocal(inv[:], one[:]),
                       lambda: V.tensor_tensor(act_[:], gu_bank[bank][:, 0:S], inv[:], ALU.mult),
                       lambda: V.tensor_tensor(up_[:], gu_bank[bank][:, S:2 * S], act_[:], ALU.mult),
                       lambda: V.tensor_tensor(full[:], share_bank[bank], up_[:], ALU.mult),
                       lambda: V.tensor_copy(h[0][:, m, :], full[:])]
                for i, op in enumerate(ops):
                    op().then_inc(step, 1)
                    dve.wait_ge(step, STEPS * n + i + 1)
                V.tensor_tensor(h[1][:, m, :], full[:], h[0][:, m, :].bitcast(F32), ALU.subtract).then_inc(h_ready, 1)

            def output(b):
                dve.wait_ge(down_ready, b + 1)
                for t in range(T):
                    res = k.res[:, bass.ds(T * b + t, 1), :].rearrange("p o d -> p (o d)")
                    V.tensor_tensor(res, down_bank[t], res, ALU.add).then_inc(y_ready, 1)
                dve.wait_ge(y_ready, T * (b + 1))
                dve.sem_inc(down_free, 1)

            gate(0, 0)
            gate(0, 1)
            with dve.Fori(0, B - 1) as b:
                for i, m in turn_slots(False):
                    gate(b + i, m)
                output(b)
            for i, m in turn_slots(True):
                if i == 0:
                    gate(B - 1, m)
            output(B - 1)


def finish(nc, k):
    k.x_loaded = k.sem("x_loaded")
    k.att_free = k.sem("att_free")
    k.gT, k.uT = ([k.at(f"{n}T_{p}", [P, C, F], AT_V + 14 * KB * (2 * i + j), F32R) for j, p in enumerate(("hi", "lo"))]
                  for i, n in enumerate(("g", "u")))
    k.dT = [k.at(f"dT_{p}", [P, FC, D], AT_V + 14 * KB * (4 + j), F32R) for j, p in enumerate(("hi", "lo"))]
    k.wo_part = [k.at(f"wo_{p}", [P, C, D], AT_V + (84 + 8 * j) * KB, F32R) for j, p in enumerate(("hi", "lo"))]
    k.expand = k.at("expand", [P, F], AT_V + 100 * KB, F32R)
    k.res = k.at("res", [P, B * S // P, D], AT_V + 104 * KB)
    k.gateT = [k.at(f"gateT_{p}", [P, C, P], AT_WORK3 + (26 + 2 * j) * KB, F32R) for j, p in enumerate(("hi", "lo"))]
    prepare(nc, k)
    k.xnT = [k.at(f"xnT_{p}", [P, C, B * S], AT_RAW + 16 * KB * j, F32R) for j, p in enumerate(("hi", "lo"))]
    k.wT = k.at("wT", [P, B * S], AT_RAW + 32 * KB, F32R)
    k.band = [k.at(f"band{i}", [2 * E, F], AT_RAW + (36 + 4 * i) * KB if i == 0 else AT_WO) for i in range(2)]
    mix(nc, k)
    experts(nc, k)




def build(nc, x, ctx_4096, wq, wk, wv, wo, gate_w, u, g, d, y):
    with ExitStack() as ctx:
        k = Plan()
        k.x, k.ctx, k.wq, k.wk, k.wv, k.wo, k.gate_w, k.u, k.g, k.d, k.y = x, ctx_4096, wq, wk, wv, wo, gate_w, u, g, d, y
        psum = ctx.enter_context(nc.psum_tensor("psum", [P, 8, 512], F32))
        k.bank = psum
        fixed = k_base(nc)

        def at(name, shape, offset, dt=F32):
            return nc.alloc_sbuf_tensor_at(name, shape, dt, offset=fixed + offset)

        k.at = at
        k.ident = at("ident", [P, P], AT_IDENT)
        k.eps = at("eps", [P, 1], AT_EPS)
        k.wo_raw = at("wo_raw", [P, C, D], AT_WO)
        k.g_raw = at("g_raw", [P, FC, D], AT_RAW)
        k.u_raw = at("u_raw", [P, FC, D], AT_RAW + 4 * FC * D)
        k.d_raw = at("d_raw", [P, C, F], AT_RAW + 8 * FC * D)
        k.v = at("v", [P, 2 * B, TILES, REP * HD], AT_V)
        k.k_dram = nc.dram_tensor("k_parts", [2, GROUPS * HD, SK], F32, kind="Internal").ap()
        k.q_dram = nc.dram_tensor("q_parts", [2, B * D, S], F32, kind="Internal").ap()
        k.pv_dram = nc.dram_tensor("pv_sums", [GROUPS * P, S], F32, kind="Internal").ap()
        k.sem = lambda name: ctx.enter_context(nc.semaphore(name))
        k.ffn_loaded = k.sem("ffn_loaded")
        project(nc, k)
        attend(nc, k)
        finish(nc, k)


_INS = ['x', 'ctx_4096', 'L0_xattn_Wq', 'L0_xattn_Wk', 'L0_xattn_Wv', 'L0_xattn_Wo', 'L0_ffn_gate_w', 'L0_ffn_u',
        'L0_ffn_g', 'L0_ffn_d']
_OUTS = [((B, S, D), 'float32')]


def kernel(**inputs):
    import numpy as _np
    import concourse.bacc as _bacc
    from concourse import mybir as _mybir
    from concourse.bass_utils import run_bass_kernel_spmd as _run

    nc = _bacc.Bacc("TRN2", target_bir_lowering=False, num_devices=1)
    arrays, args = {}, []
    for name in _INS:
        a = _np.ascontiguousarray(inputs[name])
        arrays[f"in_{name}_dram"] = a
        args.append(nc.dram_tensor(f"in_{name}_dram", a.shape, _mybir.dt.from_np(a.dtype), kind="ExternalInput").ap())
    for i, (shape, dtype) in enumerate(_OUTS):
        dt = _mybir.dt.from_np(_np.dtype(dtype))
        args.append(nc.dram_tensor(f"out_{i}_dram", shape, dt, kind="ExternalOutput").ap())
    build(nc, *args)
    r = _run(nc, [arrays], core_ids=[0])
    got = tuple(r.results[0][f"out_{i}_dram"] for i in range(len(_OUTS)))
    return got[0]
```

```python
from contextlib import ExitStack

import concourse.bass as bass
from concourse import mybir

F32 = mybir.dt.float32
F32R = mybir.dt.float32r
U32 = mybir.dt.uint32
ACT = mybir.ActivationFunctionType
ALU = mybir.AluOpType
AX = mybir.AxisListType

P = 128
B, S, D = 4, 256, 512
SK = 1601
C = D // P
HEADS, KV, HD = 32, 8, 16
REP = HEADS // KV
QC = REP * S
TILES = (SK + P - 1) // P
LAST = SK - (TILES - 1) * P
GROUPS = B * KV
NQ = QC // P
PIECES = 4
PIECE = 402
STARTS = [min(i * (PIECE - 2), SK - PIECE) for i in range(PIECES)]
UNITS = NQ * PIECES
FOUR = 4
E, INTER = 16, 56
F = E * INTER
FC = F // P
EPS = 1e-5
PARTS = ((0, 0), (0, 1), (1, 0))
ZROW, MROW = 64, 96
SROWS = MROW + 2

KB = 1024
AT_IDENT, AT_EPS, AT_NUMBERS = 0, KB // 2, KB // 2 + 64
AT_ATT = KB
AT_WO = 33 * KB
AT_TURNED = 41 * KB
AT_V = 83 * KB
AT_WORK = 109 * KB
AT_RES = AT_WORK + 17 * KB
AT_XN = AT_RES + 16 * KB
AT_WT = AT_XN + 32 * KB
AT_GATE = 181 * KB
AT_WO_PARTS = 185 * KB
AT_GATE_RAW = 201 * KB
AT_EXPAND = 204 * KB


class Plan:
    pass


class Programs:

    def __init__(self, sync, gpsimd, tensor, scalar, vector):
        self.sync, self.gpsimd, self.tensor, self.scalar, self.vector = sync, gpsimd, tensor, scalar, vector


def k_base(nc):
    return (nc.sbuf_base + 63) // 64 * 64


def product(pe, out, lhsT, rhs, chunks, first=True, last=True):
    steps = [(p, q, c) for p, q in PARTS for c in chunks]
    for i, (p, q, c) in enumerate(steps):
        mm = pe.matmul(out, lhsT(p, c), rhs(q, c), start=first and i == 0,
                       stop=last and i == len(steps) - 1)
    return mm


def project(nc, k):
    with ExitStack() as ctx:
        base = [k_base(nc) + AT_WORK]

        def sb(name, shape, dt):
            size = 4
            for n in shape[1:]:
                size *= n
            t = nc.alloc_sbuf_tensor_at(name, shape, dt, offset=base[0])
            base[0] += (size + 63) // 64 * 64
            return t

        def sem(name):
            return ctx.enter_context(nc.semaphore(name))

        wraw = sb("wraw", [P, C, D + 2 * P], F32)
        w = [sb(f"w{n}", [P, C, D + 2 * P], F32R) for n in ("hi", "lo")]
        tok = [sb(f"tok{i}", [P, 4, D], F32) for i in range(2)]
        tokT = [[sb(f"tokT{n}{i}", [P, C, 4 * P], F32R) for n in ("hi", "lo")] for i in range(2)]
        out = [[sb(f"out{n}{i}", [P, 4 * P], F32R) for n in ("hi", "lo")] for i in range(2)]
        vT = sb("vT", [P, 4 * P], F32)
        stats = sb("stats", [P, 8, 6], F32)
        mean_var = sb("mean_var", [P, 8, 2], F32)
        std = sb("std", [P, 8], F32)
        rstd = sb("rstd", [P, 8], F32)
        band = [k.at(f"band{i}", [2 * E, F], AT_TURNED + 4 * KB * i) for i in range(2)]
        turn_bank = [k.bank[:, i, :] for i in range(4)]
        kq_bank = [k.bank[:, 4 + i, :] for i in range(2)]
        vt_bank, v_bank = k.bank[:, 6, :], k.bank[:, 7, :]

        w_loaded = [sem(f"w_loaded{i}") for i in range(3)]
        w_ready = sem("w_ready")
        w_hi_done = sem("w_hi_done")
        id_zero = sem("id_zero")
        id_ready = sem("id_ready")
        tok_loaded = [sem(f"tok_loaded{i}") for i in range(2)]
        stats_ready = sem("stats_ready")
        var_ready = sem("var_ready")
        eps_ready = sem("eps_ready")
        std_ready = sem("std_ready")
        rstd_ready = sem("rstd_ready")
        ln_done = sem("ln_done")
        turned = sem("turned")
        turn_hi = sem("turn_hi")
        turn_lo = sem("turn_lo")
        kq_ready = sem("kq_ready")
        kq_hi = sem("kq_hi")
        kq_lo = sem("kq_lo")
        stored = [sem(f"stored{i}") for i in range(2)]
        vt_ready = sem("vt_ready")
        vt_copied = sem("vt_copied")
        v_ready = sem("v_ready")
        v_free = sem("v_free")
        consts = sem("consts")

        x_tok = k.x.rearrange("b s d -> (b s) d")
        QU = 8
        X_TILES = B * S // P

        def tiles(r):
            return 4 if r < 3 else 1

        def rows(r):
            return P if r < 3 else LAST

        def first_tile(b, r):
            return X_TILES + TILES * b + 4 * r

        block = ctx.enter_context(nc.Block())

        @block.sync
        def _(sp):
            for u in range(2):
                sp.dma_start(tok[u][:], x_tok[512 * u:512 * u + 512, :].rearrange("(t p) d -> p t d", p=P)
                             ).then_inc(tok_loaded[u], 16)
                if u == 0:
                    sp.dma_start(wraw[:, :, 0:D], k.wq.rearrange("(c p) n -> p c n", p=P)).then_inc(w_loaded[0], 16)
            sp.dma_start(wraw[:, :, D:D + P], k.wk.rearrange("(c p) n -> p c n", p=P)).then_inc(w_loaded[1], 16)
            sp.dma_start(wraw[:, :, D + P:], k.wv.rearrange("(c p) n -> p c n", p=P)).then_inc(w_loaded[2], 16)

            def load(b, r):
                if isinstance(b, int) and b == 0 and r < 2:
                    sp.wait_ge(turned, 4 * (r + 1))
                elif r < 2:
                    sp.wait_ge(turned, first_tile(b - 1, r + 2) + tiles(r + 2))
                else:
                    sp.wait_ge(turned, first_tile(b, r - 2) + 4)
                src = k.ctx[bass.ds(b, 1), 512 * r:512 * r + P * (tiles(r) - 1) + rows(r), :]
                sp.dma_start(tok[r % 2][0:rows(r), 0:tiles(r), :],
                             src.rearrange("o (t p) d -> p (o t) d", p=rows(r))).then_inc(tok_loaded[r % 2], 16)

            def store_k(b, r):
                sp.wait_ge(kq_lo, QU + 4 * b + r + 1)
                n = P * (tiles(r) - 1) + rows(r)
                for part in range(2):
                    sp.dma_start(k.k_dram[part, bass.ds(P * b, P), 512 * r:512 * r + n],
                                 out[r % 2][part][:, 0:n].bitcast(F32)).then_inc(stored[r % 2], 16)

            def store_q(u):
                for m in range(C):
                    sp.wait_ge(kq_lo, 4 * u + m + 1)
                    for part in range(2):
                        dst = k.q_dram[part, 2 * D * u:2 * D * (u + 1), :].rearrange("(b n) q -> n b q", b=2)
                        sp.dma_start(dst[P * m:P * (m + 1)], out[m % 2][part][:].bitcast(F32)
                                     .rearrange("p (b q) -> p b q", b=2)).then_inc(stored[m % 2], 16)

            load(0, 0)
            load(0, 1)
            store_q(0)
            load(0, 2)
            store_q(1)
            load(0, 3)
            store_k(0, 0)
            with sp.Fori(1, B) as b:
                load(b, 0)
                store_k(b - 1, 1)
                load(b, 1)
                store_k(b - 1, 2)
                load(b, 2)
                store_k(b - 1, 3)
                load(b, 3)
                store_k(b, 0)
            for raw, w_dram in ((k.g_raw, k.g), (k.u_raw, k.u)):
                sp.dma_start(raw[:], w_dram.rearrange("(m p) d -> p m d", p=P)).then_inc(k.gu_loaded, 16)
            for r in range(1, 4):
                store_k(B - 1, r)
            for i in range(2):
                sp.wait_ge(stored[i], 32 * (QU // 2 + 2 * B))

        @block.gpsimd
        def _(pool):
            nc.gpsimd.memset(k.ident[:], 0.0).then_inc(id_zero, 1)
            pool.wait_ge(id_zero, 1)
            nc.gpsimd.affine_select(out=k.ident[:], in_=k.ident[:], compare_op=ALU.not_equal, fill=1.0, base=0,
                                    pattern=[[-1, P]], channel_multiplier=1).then_inc(id_ready, 1)
            for i, (lo, hi) in enumerate(((0, D), (D, D + P), (D + P, D + 2 * P))):
                pool.wait_ge(w_loaded[i], 16)
                nc.gpsimd.tensor_copy(w[0][:, :, lo:hi], wraw[:, :, lo:hi]).then_inc(w_hi_done, 1)
                pool.wait_ge(w_hi_done, i + 1)
                nc.gpsimd.tensor_tensor(w[1][:, :, lo:hi], wraw[:, :, lo:hi], w[0][:, :, lo:hi].bitcast(F32),
                                        ALU.subtract).then_inc(w_ready, 1)
            nc.gpsimd.memset(k.expand[:].bitcast(F32), 0.0).then_inc(consts, 1)
            nc.gpsimd.iota(k.expert_no[:], [[1, E]], base=0, channel_multiplier=0,
                           allow_small_or_imprecise_dtypes=True).then_inc(consts, 1)
            for i in range(2):
                nc.gpsimd.memset(band[i][:], 0.5).then_inc(consts, 1)
            pool.wait_ge(consts, 4)
            for i in range(2):
                nc.gpsimd.affine_select(out=band[i][:], in_=band[i][:], compare_op=ALU.is_ge, fill=0.0,
                                        base=INTER * E * i, pattern=[[1, F]], channel_multiplier=-INTER
                                        ).then_inc(consts, 1)
                pool.wait_ge(consts, 5 + 2 * i)
                nc.gpsimd.affine_select(out=band[i][:], in_=band[i][:], compare_op=ALU.is_ge, fill=0.0,
                                        base=INTER - 1 - INTER * E * i, pattern=[[-1, F]], channel_multiplier=INTER
                                        ).then_inc(consts, 1)
                pool.wait_ge(consts, 6 + 2 * i)
            nc.gpsimd.tensor_tensor(k.expand[0:2 * E, :], band[0][:], band[1][:], ALU.add).then_inc(consts, 1)

        @block.tensor
        def _(pe):
            def turn(slot, tile0, n, np_):
                for j in range(n):
                    t = tile0 + j
                    if not (isinstance(t, int) and t < 4):
                        pe.wait_ge(turn_lo, t - 3)
                    for c in range(C):
                        mm = pe.transpose(turn_bank[j % 4][:, P * c:P * c + np_], tok[slot][0:np_, j, P * c:P * (c + 1)],
                                          k.ident[0:np_, 0:np_])
                    mm.then_inc(turned, 1)

            def turn_x(u):
                for j in range(4):
                    t = 4 * u + j
                    pe.wait_ge(ln_done, t + 1)
                    if t >= 4:
                        pe.wait_ge(turn_lo, t - 3)
                    for c in range(C):
                        mm = pe.transpose(turn_bank[j][:, P * c:P * (c + 1)], tok[u][:, j, P * c:P * (c + 1)], k.ident[:])
                    mm.then_inc(turned, 1)

            def turn_ctx(b, r):
                pe.wait_ge(tok_loaded[r % 2], 16 * (2 + 2 * b + r // 2))
                if r == 0:
                    pe.wait_ge(turn_lo, first_tile(b, 0))
                turn(r % 2, first_tile(b, r), tiles(r), rows(r))

            def q_of(u):
                pe.wait_ge(turn_lo, 4 * (u + 1))
                pe.wait_ge(w_ready, 1)
                for m in range(C):
                    n = 4 * u + m
                    if n >= 2:
                        pe.wait_ge(kq_lo, n - 1)
                    product(pe, kq_bank[n % 2], lambda p, c: w[p][:, c, P * m:P * (m + 1)],
                            lambda p, c: tokT[u][p][:, c, :], range(C)).then_inc(kq_ready, 1)

            def kv_of(b, r):
                n, np_ = tiles(r), rows(r)
                pe.wait_ge(turn_lo, first_tile(b, r) + n)
                cols = P * (n - 1) + np_ + np_ % 2
                product(pe, vt_bank[:, 0:cols], lambda p, c: w[p][:, c, D + P:D + 2 * P],
                        lambda p, c: tokT[r % 2][p][:, c, 0:cols], range(C)).then_inc(vt_ready, 1)
                pe.wait_ge(kq_lo, QU + 4 * b + r - 1)
                product(pe, kq_bank[r % 2][:, 0:cols], lambda p, c: w[p][:, c, D:D + P],
                        lambda p, c: tokT[r % 2][p][:, c, 0:cols], range(C)).then_inc(kq_ready, 1)
                pe.wait_ge(vt_copied, 4 * b + r + 1)
                pe.wait_ge(v_free, 4 * b + r + 1)
                for j in range(n):
                    mm = pe.transpose(v_bank[0:np_, P * j:P * (j + 1)], vT[:, P * j:P * j + np_], k.ident[:])
                mm.then_inc(v_ready, 1)

            pe.wait_ge(id_ready, 1)
            turn_x(0)
            turn_x(1)
            q_of(0)
            turn_ctx(0, 0)
            q_of(1)
            pe.wait_ge(w_ready, 3)
            with pe.Fori(0, B - 1) as b:
                for r in range(4):
                    turn_ctx(b + (r + 1) // 4, (r + 1) % 4)
                    kv_of(b, r)
            for r in range(4):
                if r < 3:
                    turn_ctx(B - 1, r + 1)
                kv_of(B - 1, r)

        @block.scalar
        def _(act):
            act.sem_inc(v_free, 1)

            def turn_part(slot, j, t, np_):
                act.wait_ge(turned, t + 1)
                src = turn_bank[j % 4].rearrange("p (c n) -> p c n", c=C)[:, :, 0:np_]
                nc.scalar.activation(tokT[slot][0][:, :, P * j:P * j + np_], src, ACT.Copy).then_inc(turn_hi, 1)

            def turn_x(u):
                for j in range(4):
                    turn_part(u, j, 4 * u + j, P)

            def turn_ctx(b, r):
                if isinstance(b, int) and b == 0 and r == 0:
                    act.wait_ge(kq_ready, 4)
                else:
                    act.wait_ge(kq_ready, QU + 4 * b + r - 1)
                for j in range(tiles(r)):
                    turn_part(r % 2, j, first_tile(b, r) + j, rows(r))

            def q_of(u):
                for m in range(C):
                    n = 4 * u + m
                    act.wait_ge(kq_ready, n + 1)
                    if n >= 2:
                        act.wait_ge(stored[n % 2], 32 * (n // 2))
                    nc.scalar.activation(out[n % 2][0][:], kq_bank[n % 2], ACT.Copy).then_inc(kq_hi, 1)

            def kv_of(b, r):
                n, np_ = tiles(r), rows(r)
                cols = P * (n - 1) + np_
                act.wait_ge(vt_ready, 4 * b + r + 1)
                nc.scalar.activation(vT[:, 0:cols], vt_bank[:, 0:cols], ACT.Copy).then_inc(vt_copied, 1)
                act.wait_ge(kq_ready, QU + 4 * b + r + 1)
                act.wait_ge(stored[r % 2], 32 * (QU // 2 + 2 * b + r // 2))
                nc.scalar.activation(out[r % 2][0][:, 0:cols], kq_bank[r % 2][:, 0:cols], ACT.Copy).then_inc(kq_hi, 1)
                act.wait_ge(v_ready, 4 * b + r + 1)
                dst = k.v[0:np_, bass.ds(2 * b, 2), 4 * r:4 * r + n, :].rearrange("p h t d -> p t h d")
                src = v_bank[0:np_, 0:P * n].rearrange("p (t h d) -> p t h d", t=n, h=2)
                nc.scalar.activation(dst, src, ACT.Copy).then_inc(v_free, 1)

            act.wait_ge(eps_ready, 1)
            for u in range(2):
                act.wait_ge(var_ready, 4 * (u + 1))
                nc.scalar.activation(std[:, 4 * u:4 * u + 4], mean_var[:, 4 * u:4 * u + 4, 1], ACT.Sqrt,
                                     bias=k.eps[:]).then_inc(std_ready, 1)
            turn_x(0)
            turn_x(1)
            q_of(0)
            turn_ctx(0, 0)
            q_of(1)
            with act.Fori(0, B - 1) as b:
                for r in range(4):
                    turn_ctx(b + (r + 1) // 4, (r + 1) % 4)
                    kv_of(b, r)
            for r in range(4):
                if r < 3:
                    turn_ctx(B - 1, r + 1)
                kv_of(B - 1, r)

        @block.vector
        def _(dve):
            def turn_part(slot, j, t, np_):
                dve.wait_ge(turn_hi, t + 1)
                src = turn_bank[j % 4].rearrange("p (c n) -> p c n", c=C)[:, :, 0:np_]
                hi, lo = (tokT[slot][p][:, :, P * j:P * j + np_] for p in range(2))
                nc.vector.tensor_tensor(lo, src, hi.bitcast(F32), ALU.subtract).then_inc(turn_lo, 1)

            def turn_ctx(b, r):
                for j in range(tiles(r)):
                    turn_part(r % 2, j, first_tile(b, r) + j, rows(r))

            def kq_part(n, slot, cols):
                dve.wait_ge(kq_hi, n + 1)
                nc.vector.tensor_tensor(out[slot][1][:, 0:cols], kq_bank[slot][:, 0:cols],
                                        out[slot][0][:, 0:cols].bitcast(F32), ALU.subtract).then_inc(kq_lo, 1)

            def q_of(u):
                for m in range(C):
                    kq_part(4 * u + m, m % 2, 4 * P)

            def kv_of(b, r):
                kq_part(QU + 4 * b + r, r % 2, P * (tiles(r) - 1) + rows(r))

            nc.vector.memset(k.eps[:], EPS).then_inc(eps_ready, 1)
            for u in range(2):
                dve.wait_ge(tok_loaded[u], 16)
                for j in range(4):
                    nc.vector.bn_stats(stats[:, 4 * u + j, :], tok[u][:, j, :]).then_inc(stats_ready, 1)
                dve.wait_ge(stats_ready, 4 * (u + 1))
                for j in range(4):
                    nc.vector.bn_aggr(mean_var[:, 4 * u + j, :], stats[:, 4 * u + j, :]).then_inc(var_ready, 1)
                dve.wait_ge(std_ready, u + 1)
                nc.vector.reciprocal(rstd[:, 4 * u:4 * u + 4], std[:, 4 * u:4 * u + 4]).then_inc(rstd_ready, 1)
                dve.wait_ge(rstd_ready, u + 1)
                for j in range(4):
                    nc.vector.tensor_scalar(tok[u][:, j, :], tok[u][:, j, :], mean_var[:, 4 * u + j, 0:1],
                                            rstd[:, 4 * u + j:4 * u + j + 1], ALU.subtract, ALU.mult
                                            ).then_inc(ln_done, 1)
            for u in range(2):
                for j in range(4):
                    turn_part(u, j, 4 * u + j, P)
            q_of(0)
            turn_ctx(0, 0)
            q_of(1)
            with dve.Fori(0, B - 1) as b:
                for r in range(4):
                    turn_ctx(b + (r + 1) // 4, (r + 1) % 4)
                    kv_of(b, r)
            for r in range(4):
                if r < 3:
                    turn_ctx(B - 1, r + 1)
                kv_of(B - 1, r)


def attend(nc, k):
    base = [k_base(nc) + AT_WORK]

    def sb(name, shape, dt):
        size = 4
        for n in shape[1:]:
            size *= n
        t = nc.alloc_sbuf_tensor_at(name, shape, dt, offset=base[0])
        base[0] += (size + 63) // 64 * 64
        return t

    def sem(name):
        return k.sem(name)

    ks, qs = [None] * FOUR, [None] * FOUR
    ks[0], ks[1] = (sb(f"ks{i}", [P, SK], F32R) for i in range(2))
    qs[0], qs[1] = (sb(f"qs{i}", [P, QC], F32R) for i in range(2))
    ks[2], qs[2] = sb("ks2", [P, SK], F32R), sb("qs2", [P, QC], F32R)
    piece_max = [sb(f"piece_max{i}", [P, UNITS], F32) for i in range(2)]
    neg_max = [sb(f"neg_max{i}", [P, NQ], F32) for i in range(2)]
    max_hi = [sb(f"max_hi{i}", [NQ, P], F32R) for i in range(2)]
    max_lo = [sb(f"max_lo{i}", [NQ, P], F32R) for i in range(2)]
    assert base[0] - k_base(nc) >= AT_XN
    ks[3], qs[3] = sb("ks3", [P, SK], F32R), sb("qs3", [P, QC], F32R)
    vg = [sb(f"vg{i}", [P, TILES, 2 * HD], F32) for i in range(2)]
    probs = [sb(f"probs{i}", [P, QC], F32) for i in range(FOUR)]
    pv = [sb(f"pv{i}", [P, S], F32) for i in range(2)]
    sums = sb("sums", [P, FOUR * QC // P], F32)
    inv_sums = sb("inv_sums", [P, FOUR * QC // P], F32)
    inv = sb("inv", [P, 2, S], F32)
    att = sb("att", [P, 2, S], F32)
    tick = sb("tick", [P, 1], F32)
    assert base[0] - k_base(nc) <= AT_GATE
    d_raw = k.at("d_raw", [P, C, F], AT_WO_PARTS)
    gate_raw = k.at("gate_raw", [E, D], AT_GATE_RAW)
    score_bank = [k.bank[:, 2 * i:2 * i + 2, :].rearrange("p b n -> p (b n)") for i in range(2)]
    pv_bank = k.bank[:, 4, 0:S]
    row_bank = [k.bank[:, 5 + i, :] for i in range(3)]

    fixed_rows = sem("fixed_rows")
    loaded = [sem(f"qk_loaded{i}") for i in range(FOUR)]
    max_loaded = [sem(f"max_loaded{i}") for i in range(FOUR)]
    rows_ready = sem("rows_ready")
    rows_free = sem("rows_free")
    max_ready = sem("max_ready")
    max_split = sem("max_split")
    scores_ready = sem("scores_ready")
    probs_ready = sem("probs_ready")
    v_ready = sem("vg_ready")
    pv_done = sem("pv_done")
    pv_free = sem("pv_free")
    pv_moved = [sem(f"pv_moved{i}") for i in range(2)]
    sums_loaded = sem("sums_loaded")
    inv_ready = sem("inv_ready")
    inv_stored = sem("inv_stored")
    inv_loaded = sem("inv_loaded")
    att_ready, att_hi, att_lo = sem("att_ready"), sem("att_hi"), sem("att_lo")
    d_loaded, gate_loaded, wo_loaded = sem("d_loaded"), sem("gate_loaded"), sem("wo_loaded")
    turned = sem("w_turned")
    copied = sem("w_copied")
    gate_lo = sem("gate_lo")
    wo_hi, wo_lo = sem("wo_hi"), sem("wo_lo")
    w_hi, w_lo = sem("w_hi"), sem("w_lo")

    TURNS = GROUPS // FOUR
    MOVES = 16 * (REP + 1)
    FIXED = 3 * FOUR + 4
    AHEAD = TILES + 6
    PER_TURN = FOUR * (UNITS + 1)

    def keys(t):
        return P if t < TILES - 1 else LAST

    def units(part):
        return range(UNITS * part // TILES, UNITS * (part + 1) // TILES)

    def row_steps(g, i, t, last):
        ahead, part = divmod(t + AHEAD - TILES, TILES)
        g, i = g + 1 + ahead, i + 1 + ahead
        steps = []
        for u in units(part):
            if u == 3 and not (last and i > FOUR):
                steps.append((g - 1, i - 1, "max"))
            if not (last and i >= FOUR):
                steps.append((g, i, u))
        return steps

    def index(g, step, last=False):
        if step == "max":
            return (UNITS + 1) * (g + 1) + (2 if not last else -1)
        if isinstance(g, int) and g == 0:
            return step
        return (UNITS + 1) * g - 1 + step + (step >= 3)

    def bank_of(g, step):
        return row_bank[index(0 if step == "max" or (isinstance(g, int) and g == 0) else 3, step) % 3]

    def first_rows(do):
        for u in range(UNITS):
            do(0, 0, u)
        for part in range(AHEAD - TILES):
            for u in units(part):
                if u == 3:
                    do(0, 0, "max")
                do(1, 1, u)

    W_UNITS = 3 * FC + 1

    def raw_blocks(n):
        m = n % FC
        if n < 2 * FC:
            return [(k.g_raw, k.u_raw)[n // FC][:, m, P * c:P * (c + 1)] for c in range(C)]
        if n < 3 * FC:
            return [d_raw[:, c, P * m:P * (m + 1)] for c in range(C)]
        return [gate_raw[:, P * c:P * (c + 1)] for c in range(C)]

    def turned_home(n):
        m = n % FC
        if n < 2 * FC:
            return (k.gT_full, k.uT_full)[n // FC][:, :, P * m:P * (m + 1)]
        if n < 3 * FC:
            return k.dT_full[:, m, :].rearrange("p (c n) -> p c n", c=C)
        return k.gateT[0][:, :, 0:E]

    def width(n):
        return P if n < 3 * FC else E

    def turned_bank(n):
        return k.bank[:, n % 4, 0:C * width(n)]

    def turn_slots(last):
        return [divmod(s, TILES) for s in range(1, FOUR * TILES + (0 if last else 1))]

    def gpsimd(pool):
        for i in range(FOUR):
            nc.gpsimd.memset(ks[i][ZROW:MROW, :].bitcast(F32), 0.0).then_inc(fixed_rows, 1)
            nc.gpsimd.memset(ks[i][MROW:SROWS, :].bitcast(F32), 1.0).then_inc(fixed_rows, 1)
            nc.gpsimd.memset(qs[i][ZROW:MROW, :].bitcast(F32), 0.0).then_inc(fixed_rows, 1)
        pool.wait_ge(fixed_rows, 3 * FOUR)
        for i in range(2):
            nc.gpsimd.memset(vg[i][:, :, HD:], 1.0).then_inc(fixed_rows, 1)
        for p in range(2):
            nc.gpsimd.memset(k.gateT[p][:, :, E:].bitcast(F32), 0.0).then_inc(fixed_rows, 1)

        def copy(h, i):
            for rows, t0, t1 in ((P, 0, TILES - 1), (LAST, TILES - 1, TILES)):
                src = k.v[0:rows, bass.ds(h + i // FOUR, 1), t0:t1, HD * (i % FOUR):HD * (i % FOUR + 1)]
                nc.gpsimd.tensor_copy(vg[i % 2][0:rows, t0:t1, 0:HD],
                                      src.rearrange("p o t d -> p (o t) d")).then_inc(v_ready, 1)

        def after():
            nc.gpsimd.tensor_tensor(tick[:], k.eps[:], k.eps[:], ALU.add)

        def divide(h):
            here = [x[:, bass.ds(2 * h, 2), :] for x in k.att]
            pool.wait_ge(att_lo, h + 1)
            pool.wait_ge(inv_loaded, 32 * (h + 1))
            after()
            nc.gpsimd.tensor_tensor(att[:], here[1].bitcast(F32), inv[:], ALU.mult).then_inc(att_ready, 1)
            pool.wait_ge(att_ready, h + 2)
            nc.gpsimd.tensor_copy(here[0], att[:]).then_inc(att_hi, 1)
            pool.wait_ge(att_hi, h + 1)
            after()
            nc.gpsimd.tensor_tensor(here[1], att[:], here[0].bitcast(F32), ALU.subtract).then_inc(att_lo, 1)

        pool.sem_inc(att_ready, 1)
        pool.sem_inc(att_lo, 1)
        copy(0, 0)
        copy(0, 1)
        pool.wait_ge(wo_loaded, 16)
        pool.wait_ge(copied, 3 * FC)
        nc.gpsimd.tensor_copy(k.wo_part[0][:], k.wo_raw[:]).then_inc(wo_hi, 1)
        pool.wait_ge(wo_hi, 1)
        nc.gpsimd.tensor_tensor(k.wo_part[1][:], k.wo_raw[:], k.wo_part[0][:].bitcast(F32), ALU.subtract
                                ).then_inc(wo_lo, 1)

        def copy_next(h, i):
            pool.wait_ge(pv_done, TILES * (FOUR * h + i + 1))
            copy(h, i + 2)

        for i in range(FOUR):
            copy_next(0, i)
        with pool.Fori(1, TURNS - 1) as h:
            for i in range(FOUR):
                copy_next(h, i)
                if i == 2:
                    divide(h - 1)
        for i in range(FOUR - 2):
            copy_next(TURNS - 1, i)
        divide(TURNS - 2)
        divide(TURNS - 1)

    def sync(sp):
        def load(h, i):
            g = FOUR * h + i
            for part in range(2):
                sp.dma_start(ks[i][2 * HD * part:2 * HD * (part + 1), :].bitcast(F32),
                             k.k_dram[part, bass.ds(HD * g, HD), :].partition_broadcast(2)
                             ).then_inc(loaded[i], 16)
                src = k.q_dram[part, bass.ds(REP * HD * g, REP * HD), :].rearrange("(h d) q -> d h q", h=REP)
                for row in (HD * part, HD * (part + 2)):
                    sp.dma_start(qs[i][row:row + HD, :].bitcast(F32).rearrange("d (h q) -> d h q", h=REP),
                                 src).then_inc(loaded[i], 16)

        def put_max(g, i, last=False):
            sp.wait_ge(rows_free, index(g, "max", last) + 1 + 3)
            for n, src in enumerate((max_hi, max_lo)):
                row = MROW + n
                sp.dma_start(qs[i % FOUR][row:row + 1, :].bitcast(F32).rearrange("o (j q) -> o j q", j=NQ),
                             src[i % 2][:].bitcast(F32)).then_inc(max_loaded[i % FOUR], 16)

        def put_pv(h, i):
            sp.wait_ge(pv_free, FOUR * h + i + 2)
            for j in range(REP):
                row = 64 * (i % 2) + HD * j
                sp.dma_start(k.att[1][row:row + HD, bass.ds(2 * h + i // 2, 1), :].bitcast(F32)
                             .rearrange("p o q -> p (o q)"), pv[i % 2][32 * j:32 * j + HD, :]
                             ).then_inc(pv_moved[i % 2], 16)
            if i == 0:
                sp.wait_ge(sums_loaded, 16 * (h + 1))
            sp.dma_start(k.sums_dram[REP * i:REP * (i + 1), :], pv[i % 2][HD::32, :]).then_inc(pv_moved[i % 2], 16)

        def load_sums(h):
            for i in range(2):
                sp.wait_ge(pv_moved[i], MOVES * (2 * h + 3))
            sp.wait_ge(inv_ready, h + 1)
            sp.dma_start(sums[:], k.sums_dram.rearrange("(a n) (b q) -> (a n b) q", a=2, b=8)
                         ).then_inc(sums_loaded, 16)

        def replicate(h):
            sp.wait_ge(inv_ready, h + 2)
            sp.wait_ge(att_ready, h + 1)
            sp.dma_start(k.inv_dram.rearrange("(a n) (b q) -> (a n b) q", a=2, b=8), inv_sums[:]
                         ).then_inc(inv_stored, 16)
            sp.wait_ge(inv_stored, 16 * (h + 1))
            for c in range(2):
                src = k.inv_dram[8 * c:8 * (c + 1), :].unsqueeze(1).broadcast_to([8, HD, S])
                sp.dma_start(inv[:, c, :], src).then_inc(inv_loaded, 16)

        load(0, 0)
        sp.dma_start(d_raw[:], k.d.rearrange("(c p) f -> p c f", p=P)).then_inc(d_loaded, 16)
        load(0, 1)
        sp.dma_start(gate_raw[:], k.gate_w).then_inc(gate_loaded, 16)
        load(0, 2)
        load(0, 3)
        sp.dma_start(k.wo_raw[:], k.wo.rearrange("(c p) n -> p c n", p=P)).then_inc(wo_loaded, 16)
        put_max(0, 0)

        def group(h, i, first):
            put_max(FOUR * h + i + 1, i + 1)
            sp.wait_ge(scores_ready, TILES * (FOUR * h + i + 1))
            load(h + 1, i)
            if i == 1 and not first:
                replicate(h - 1)
            put_pv(h, i)

        for i in range(FOUR):
            group(0, i, True)
        load_sums(0)
        with sp.Fori(1, TURNS - 1) as h:
            for i in range(FOUR):
                group(h, i, False)
            load_sums(h)
        for i in range(FOUR):
            if i < FOUR - 1:
                put_max(GROUPS - FOUR + i + 1, i + 1, last=i == FOUR - 2)
            if i == 1:
                replicate(TURNS - 2)
            if i == FOUR - 1:
                sp.wait_ge(scores_ready, TILES * (GROUPS - 1) + 1)
                sp.dma_start(k.res[:], k.x.rearrange("b (t p) d -> p (b t) d", p=P)).then_inc(k.x_loaded, 16)
            put_pv(TURNS - 1, i)
        load_sums(TURNS - 1)
        replicate(TURNS - 1)
        sp.wait_ge(inv_loaded, 32 * TURNS)

    def tensor(pe):
        def rows_step(g, i, step, last=False):
            bank = bank_of(g, step)
            if step == "max":
                pe.wait_ge(max_ready, g + 1)
            pe.wait_ge(rows_free, index(g, step, last) + 1)
            if step == "max":
                pe.transpose(bank[0:NQ, 0:P], neg_max[i % 2][:], k.ident[:]).then_inc(rows_ready, 1)
                return
            if step == 0:
                pe.wait_ge(loaded[i % FOUR], 24 * (g - i % FOUR) + 96)
            j, piece = divmod(step, PIECES)
            pe.matmul(bank[:, 0:PIECE], qs[i % FOUR][0:MROW, P * j:P * (j + 1)],
                      ks[i % FOUR][0:MROW, STARTS[piece]:STARTS[piece] + PIECE],
                      start=True, stop=True).then_inc(rows_ready, 1)

        def scores(h, i, t):
            if t == 0:
                pe.wait_ge(max_loaded[i % FOUR], 32 * (h + i // FOUR + 1))
            s = TILES * i + t
            for half in range(2):
                mm = pe.matmul(score_bank[s % 2][0:keys(t), 512 * half:512 * (half + 1)],
                               ks[i % FOUR][0:SROWS, P * t:P * t + keys(t)],
                               qs[i % FOUR][0:SROWS, 512 * half:512 * (half + 1)], start=True, stop=True)
            mm.then_inc(scores_ready, 1)

        def p_v(h, i, t):
            g, s = FOUR * h + i, TILES * i + t
            pe.wait_ge(probs_ready, TILES * g + t + 1)
            if t == 0:
                pe.wait_ge(v_ready, 2 * (g + 1))
                pe.wait_ge(pv_free, g + 1)
            for j in range(REP):
                mm = pe.matmul(pv_bank[32 * j:32 * (j + 1), :], vg[i % 2][0:keys(t), t, :],
                               probs[s % FOUR][0:keys(t), S * j:S * (j + 1)],
                               start=t == 0, stop=t == TILES - 1)
            mm.then_inc(pv_done, 1)

        def slot(h, i, t, last):
            scores(h, i, t)
            for g, ii, step in row_steps(FOUR * h + i, i, t, last):
                rows_step(g, ii, step, last and ii == FOUR - 1)
            p_v(h, *divmod(TILES * i + t - 1, TILES))

        def turn_weights(n):
            for at, loaded_sem, count in ((0, k.gu_loaded, 32), (2 * FC, d_loaded, 16), (3 * FC, gate_loaded, 16)):
                if n == at:
                    pe.wait_ge(loaded_sem, count)
            if n >= 4:
                pe.wait_ge(copied, n - 3)
            w = width(n)
            for c, blk in enumerate(raw_blocks(n)):
                mm = pe.transpose(turned_bank(n)[:, w * c:w * (c + 1)], blk, k.ident[0:w, 0:w])
            mm.then_inc(turned, 1)

        def row_and_weights(g, i, step):
            if g == 0 and step != "max" and 8 <= step < 8 + W_UNITS:
                turn_weights(step - 8)
            rows_step(g, i, step)

        pe.wait_ge(fixed_rows, FIXED)
        first_rows(row_and_weights)
        pe.wait_ge(copied, W_UNITS)
        pe.wait_ge(gate_lo, 1)
        scores(0, 0, 0)
        for g, ii, step in row_steps(0, 0, 0, False):
            rows_step(g, ii, step)
        with pe.Fori(0, TURNS - 1) as h:
            for i, t in turn_slots(False):
                slot(h, i, t, False)
        for i, t in turn_slots(True):
            slot(TURNS - 1, i, t, True)
        p_v(TURNS - 1, FOUR - 1, TILES - 1)

    def scalar(act):
        act.sem_inc(pv_free, 1)
        for i in range(2):
            act.sem_inc(pv_moved[i], MOVES)
        for n in range(W_UNITS):
            act.wait_ge(turned, n + 1)
            nc.scalar.activation(turned_home(n), turned_bank(n).rearrange("p (c n) -> p c n", c=C), ACT.Copy
                                 ).then_inc(copied, 1)

        def exponential(h, i, t):
            s = TILES * i + t
            act.wait_ge(scores_ready, TILES * FOUR * h + s + 1)
            nc.scalar.activation(probs[s % FOUR][0:keys(t), :], score_bank[s % 2][0:keys(t), :], ACT.Exp,
                                 scale=HD ** -0.5).then_inc(probs_ready, 1)

        def take_pv(h, i):
            g = FOUR * h + i
            act.wait_ge(pv_done, TILES * (g + 1))
            act.wait_ge(pv_moved[i % 2], MOVES * (2 * h + i // 2 + 1))
            nc.scalar.activation(pv[i % 2][:], pv_bank, ACT.Copy).then_inc(pv_free, 1)

        exponential(0, 0, 0)
        with act.Fori(0, TURNS - 1) as h:
            for i, t in turn_slots(False):
                exponential(h, i, t)
                if t == 0:
                    take_pv(h, i - 1)
        for i, t in turn_slots(True):
            exponential(TURNS - 1, i, t)
            if t == 0:
                take_pv(TURNS - 1, i - 1)
        take_pv(TURNS - 1, FOUR - 1)

    def invert(dve, turns):
        dve.wait_ge(sums_loaded, 16 * turns + 16)
        nc.vector.reciprocal(inv_sums[:], sums[:]).then_inc(inv_ready, 1)

    def vector(dve):
        dve.sem_inc(rows_free, 3)

        def rows_step(g, i, step, last=False):
            bank, n = bank_of(g, step), index(g, step, last)
            dve.wait_ge(rows_ready, n + 1)
            if step == "max":
                nc.vector.tensor_copy(max_hi[i % 2][:], bank[0:NQ, 0:P]).then_inc(max_split, 1)
                dve.wait_ge(max_split, g + 1)
                nc.vector.tensor_tensor(max_lo[i % 2][:], bank[0:NQ, 0:P], max_hi[i % 2][:].bitcast(F32),
                                        ALU.subtract).then_inc(rows_free, 1)
                return
            nc.vector.tensor_reduce(piece_max[i % 2][:, step:step + 1], bank[:, 0:PIECE], AX.X, ALU.max
                                    ).then_inc(rows_free, 1)
            if step == UNITS - 1:
                dve.wait_ge(rows_free, n + 1 + 3)
                nc.vector.tensor_reduce(neg_max[i % 2][:], piece_max[i % 2][:].rearrange("p (j c) -> p j c", c=PIECES),
                                        AX.X, ALU.max, negate=True).then_inc(max_ready, 1)

        nc.vector.memset(sums[:], 1.0).then_inc(sums_loaded, 16)
        first_rows(rows_step)
        n = W_UNITS - 1
        dve.wait_ge(copied, W_UNITS)
        nc.vector.tensor_tensor(k.gateT[1][:, :, 0:E], turned_bank(n).rearrange("p (c n) -> p c n", c=C),
                                k.gateT[0][:, :, 0:E].bitcast(F32), ALU.subtract).then_inc(gate_lo, 1)
        for g, ii, step in row_steps(0, 0, 0, False):
            rows_step(g, ii, step)
        with dve.Fori(0, TURNS - 1) as h:
            for i, t in turn_slots(False):
                for g, ii, step in row_steps(FOUR * h + i, i, t, False):
                    rows_step(g, ii, step)
                if (i, t) == (0, 8):
                    invert(dve, h)
        for i, t in turn_slots(True):
            for g, ii, step in row_steps(FOUR * (TURNS - 1) + i, i, t, True):
                rows_step(g, ii, step, ii == FOUR - 1)
            if (i, t) == (0, 8):
                invert(dve, TURNS - 1)
        dve.wait_ge(scores_ready, TILES * (GROUPS - 2))
        dve.wait_ge(v_ready, 2 * GROUPS)
        for i, (w, parts) in enumerate(((k.gT_full, k.gT), (k.uT_full, k.uT), (k.dT_full, k.dT))):
            nc.vector.tensor_copy(parts[0][:], w[:]).then_inc(w_hi, 1)
            dve.wait_ge(w_hi, i + 1)
            nc.vector.tensor_tensor(parts[1][:], w[:], parts[0][:].bitcast(F32), ALU.subtract).then_inc(w_lo, 1)

    k.att_lo, k.wo_lo, k.w_lo, k.pv_free, k.pv_moved = att_lo, wo_lo, w_lo, pv_free, pv_moved
    k.row_pieces = rows_free, index(GROUPS - 1, UNITS - 1, True) + 1 + 3
    k.all_moved = MOVES * (2 * TURNS + 1)
    k.invert_last = lambda dve: invert(dve, TURNS)
    return Programs(sync, gpsimd, tensor, scalar, vector)


def mix(nc, k):
    def sem(name):
        return k.sem(name)

    T = S // P
    NT = B * T
    room = {"small": AT_WO, "more": AT_GATE_RAW}

    def tiny(name, shape, dt=F32, where="small"):
        size = 4
        for n in shape[1:]:
            size *= n
        t = k.at(name, shape, room[where], dt)
        room[where] += (size + 63) // 64 * 64
        return t

    xn = [tiny(f"xn{t}", [P, D]) for t in range(2)]
    stats, mean_var = tiny("stats3", [P, NT, 6]), tiny("mean_var3", [P, NT, 2])
    std, rstd = tiny("std3", [P, NT]), tiny("rstd3", [P, NT])
    logits, top_logit = tiny("logits", [P, NT, E]), tiny("top_logit", [P, NT, 8])
    exps, total, inv_total = tiny("exps", [P, NT, E]), tiny("total", [P, NT]), tiny("inv_total", [P, NT])
    prob, top, top_at = tiny("prob", [P, NT, E]), tiny("top", [P, NT, 8]), tiny("top_at", [P, NT, 8], U32)
    two, inv_two = tiny("two", [P, NT]), tiny("inv_two", [P, NT])
    share, at_f = tiny("share", [P, NT, 2]), tiny("at_f", [P, NT, 2])
    w1, w2, w = (tiny(f"w_{n}", [P, NT, E], where="more") for n in ("first", "second", "both"))
    wparts = tiny("wparts", [P, NT, 2 * E], where="more")
    assert room["small"] <= AT_TURNED and room["more"] <= AT_EXPAND
    ltT = k.at("ltT", [E, B * S], AT_ATT)

    wo_bank = [k.bank[:, i, :] for i in range(T)]
    turn_bank = [k.bank[:, 2 + i, :] for i in range(2)]
    lt_bank = [k.bank[:, 4 + i, 0:S] for i in range(2)]
    logit_bank = k.bank[:, 3, 0:NT * E]
    wt_bank = k.bank[:, 6:8, :].rearrange("p b n -> p (b n)")

    wo_ready = sem("wo_ready")
    added = sem("added")
    stats_ready = sem("stats3_ready")
    var_ready = sem("var3_ready")
    std_ready = sem("std3_ready")
    rstd_ready = sem("rstd3_ready")
    xn_ready = sem("xn_ready")
    turned = sem("xn_turned")
    turn_hi, turn_lo = sem("xn_hi"), sem("xn_lo")
    lt_ready, lt_copied = sem("lt_ready"), sem("lt_copied")
    logit_turned, logit_ready = sem("logit_turned"), sem("logit_ready")
    less_top = sem("less_top")
    exp_ready = sem("exp_ready")
    step = sem("router_step")
    w_split = sem("w_split")
    wt_turned, wt_ready = sem("wt_turned"), sem("wt_ready")
    wt_zero = sem("wt_zero")

    def gpsimd(pool):
        pool.wait_ge(k.att_lo, GROUPS // FOUR + 1)
        nc.gpsimd.memset(k.wT[:].bitcast(F32), 0.0).then_inc(wt_zero, 1)

    def tensor(pe):
        def project_out(t):
            b, col = t // T, P * (t % T)
            if t % T == 0:
                pe.wait_ge(k.att_lo, 2 * (b + 1) + 1)
            if t >= 2:
                pe.wait_ge(added, t - 1)
            product(pe, wo_bank[t % 2], lambda p, c: k.att[p][:, C * b + c, col:col + P],
                    lambda p, c: k.wo_part[p][:, c, :], range(C)).then_inc(wo_ready, 1)

        def turn(t):
            pe.wait_ge(xn_ready, t + 1)
            if t >= 2:
                pe.wait_ge(turn_lo, t - 1)
            for c in range(C):
                mm = pe.transpose(turn_bank[t % 2][:, P * c:P * (c + 1)], xn[t % 2][:, P * c:P * (c + 1)],
                                  k.ident[:])
            mm.then_inc(turned, 1)

        def logits_of(b):
            pe.wait_ge(turn_lo, T * (b + 1))
            if b == 0:
                pe.wait_ge(k.pv_free, GROUPS + 1)
                pe.wait_ge(*k.row_pieces)
            if b >= 2:
                pe.wait_ge(lt_copied, b - 1)
            product(pe, lt_bank[b % 2], lambda p, c: k.gateT[p][:, c, :],
                    lambda p, c: k.xnT[p][:, c, S * b:S * (b + 1)], range(C)).then_inc(lt_ready, 1)

        pe.wait_ge(k.wo_lo, 1)
        project_out(0)
        project_out(1)
        for t in range(NT):
            if t + 2 < NT:
                project_out(t + 2)
            turn(t)
            if t >= 2 and t % T == 0:
                logits_of(t // T - 1)
        logits_of(B - 1)
        for b in range(B):
            pe.wait_ge(lt_copied, b + 1)
            for t in range(T * b, T * (b + 1)):
                mm = pe.transpose(logit_bank[:, E * t:E * (t + 1)], ltT[:, P * t:P * (t + 1)], k.ident[0:E, 0:E])
        mm.then_inc(logit_turned, 1)
        pe.wait_ge(k.w_lo, 3)
        for m in range(2):
            k.gate_up(pe, 0, m)
        pe.wait_ge(w_split, 1)
        for t in range(NT):
            mm = pe.transpose(wt_bank[0:2 * E, P * t:P * (t + 1)], wparts[:, t, :], k.ident[:])
        mm.then_inc(wt_turned, 1)

    def scalar(act):
        def std_of(t):
            act.wait_ge(var_ready, t + 1)
            nc.scalar.activation(std[:, t:t + 1], mean_var[:, t, 1:2], ACT.Sqrt, bias=k.eps[:]).then_inc(std_ready, 1)

        std_of(0)
        for t in range(NT):
            if t + 1 < NT:
                std_of(t + 1)
            act.wait_ge(turned, t + 1)
            nc.scalar.activation(k.xnT[0][:, :, P * t:P * (t + 1)],
                                 turn_bank[t % 2].rearrange("p (c n) -> p c n", c=C), ACT.Copy
                                 ).then_inc(turn_hi, 1)
            b = t // T - 1
            if b >= 0 and t % T == 0:
                act.wait_ge(lt_ready, b + 1)
                nc.scalar.activation(ltT[:, S * b:S * (b + 1)], lt_bank[b % 2][0:E, :], ACT.Copy
                                     ).then_inc(lt_copied, 1)
        b = B - 1
        act.wait_ge(lt_ready, b + 1)
        nc.scalar.activation(ltT[:, S * b:S * (b + 1)], lt_bank[b % 2][0:E, :], ACT.Copy).then_inc(lt_copied, 1)
        act.wait_ge(logit_turned, 1)
        nc.scalar.activation(logits[:].rearrange("p t e -> p (t e)"), logit_bank, ACT.Copy).then_inc(logit_ready, 1)
        act.wait_ge(less_top, 1)
        nc.scalar.activation(exps[:], logits[:], ACT.Exp).then_inc(exp_ready, 1)
        act.wait_ge(wt_turned, 1)
        act.wait_ge(wt_zero, 1)
        nc.scalar.activation(k.wT[0:2 * E, :], wt_bank[0:2 * E, :], ACT.Copy).then_inc(wt_ready, 1)

    def vector(dve):
        dve.wait_ge(k.x_loaded, 16)
        dve.wait_ge(k.wo_lo, 1)
        V = nc.vector

        def add(t):
            res = k.res[:, t, :]
            dve.wait_ge(wo_ready, t + 1)
            V.tensor_tensor(res, wo_bank[t % 2], res, ALU.add).then_inc(added, 1)
            dve.wait_ge(added, t + 1)
            V.bn_stats(stats[:, t, :], res).then_inc(stats_ready, 1)
            dve.wait_ge(stats_ready, t + 1)
            V.bn_aggr(mean_var[:, t, :], stats[:, t, :]).then_inc(var_ready, 1)

        def normalise(t):
            dve.wait_ge(std_ready, t + 1)
            V.reciprocal(rstd[:, t:t + 1], std[:, t:t + 1]).then_inc(rstd_ready, 1)
            dve.wait_ge(rstd_ready, t + 1)
            if t >= 2:
                dve.wait_ge(turned, t - 1)
            V.tensor_scalar(xn[t % 2][:], k.res[:, t, :], mean_var[:, t, 0:1], rstd[:, t:t + 1], ALU.subtract,
                            ALU.mult).then_inc(xn_ready, 1)

        def split(t):
            if t == 0:
                for i in range(2):
                    dve.wait_ge(k.pv_moved[i], k.all_moved)
            dve.wait_ge(turn_hi, t + 1)
            hi, lo = (k.xnT[p][:, :, P * t:P * (t + 1)] for p in range(2))
            V.tensor_tensor(lo, turn_bank[t % 2].rearrange("p (c n) -> p c n", c=C), hi.bitcast(F32),
                            ALU.subtract).then_inc(turn_lo, 1)

        add(0)
        add(1)
        normalise(0)
        k.invert_last(dve)
        for t in range(NT):
            if t + 1 < NT:
                normalise(t + 1)
            if t + 2 < NT:
                add(t + 2)
            split(t)
        done = [0]

        def mark(ins):
            done[0] += 1
            ins.then_inc(step, 1)

        def marked():
            dve.wait_ge(step, done[0])

        def over(column):
            return column.broadcast_to([P, NT, E])

        dve.wait_ge(logit_ready, 1)
        for t in range(NT):
            mark(V.max(top_logit[:, t, :], logits[:, t, :]))
        marked()
        V.tensor_tensor(logits[:], logits[:], over(top_logit[:, :, 0:1]), ALU.subtract).then_inc(less_top, 1)
        dve.wait_ge(exp_ready, 1)
        mark(V.tensor_reduce(total[:], exps[:], AX.X, ALU.add))
        marked()
        mark(V.reciprocal(inv_total[:], total[:]))
        marked()
        mark(V.tensor_tensor(prob[:], exps[:], over(inv_total[:].unsqueeze(2)), ALU.mult))
        marked()
        for t in range(NT):
            mark(V.max(top[:, t, :], prob[:, t, :]))
        marked()
        for t in range(NT):
            mark(V.max_index(top_at[:, t, :], top[:, t, :], prob[:, t, :]))
        mark(V.tensor_tensor(two[:], top[:, :, 0], top[:, :, 1], ALU.add))
        marked()
        mark(V.reciprocal(inv_two[:], two[:]))
        mark(V.tensor_copy(at_f[:], top_at[:, :, 0:2]))
        marked()
        mark(V.tensor_tensor(share[:], top[:, :, 0:2], inv_two[:].unsqueeze(2).broadcast_to([P, NT, 2]), ALU.mult))
        numbers = k.expert_no[:].unsqueeze(1).broadcast_to([P, NT, E])
        for dst, n in ((w1, 0), (w2, 1)):
            mark(V.tensor_tensor(dst[:], numbers, over(at_f[:, :, n:n + 1]), ALU.is_equal))
        marked()
        for dst, n in ((w1, 0), (w2, 1)):
            mark(V.tensor_tensor(dst[:], dst[:], over(share[:, :, n:n + 1]), ALU.mult))
        marked()
        mark(V.tensor_tensor(w[:], w1[:], w2[:], ALU.add))
        marked()
        mark(V.tensor_copy(wparts[:, :, 0:E].bitcast(F32R), w[:]))
        marked()
        V.tensor_tensor(wparts[:, :, E:], w[:], wparts[:, :, 0:E], ALU.subtract).then_inc(w_split, 1)

    k.wt_ready = wt_ready
    return Programs(None, gpsimd, tensor, scalar, vector)


def experts(nc, k):
    def sem(name):
        return k.sem(name)

    T = S // P
    h = [k.at(f"h_{n}", [P, FC, S], AT_ATT + 7 * KB * i, F32R) for i, n in enumerate(("hi", "lo"))]
    work = AT_ATT + 14 * KB
    BANK = (0, 1, 0, 1, 0, 1, 2)
    tanh = [k.at(f"tanh{i}", [P, S], work + KB * i) for i in range(3)]
    gated = k.at("gated", [P, S], work + 3 * KB)
    gated_up = k.at("gated_up", [P, S], work + 4 * KB)
    full = [k.at(f"h_full{i}", [P, S], work + KB * (5 + i)) for i in range(3)]
    gu_bank = [k.bank[:, i, :] for i in range(3)]
    share_bank = [k.bank[:, 3 + i, 0:S] for i in range(3)]
    down_bank = [k.bank[:, 6 + t, :] for t in range(T)]

    gu_ready = sem("gu_ready")
    tanh_ready = sem("tanh_ready")
    gated_ready = sem("gated_ready")
    up_ready = sem("gated_up_ready")
    full_ready = sem("h_full_ready")
    h_hi = sem("h_hi")
    h_ready = sem("h_ready")
    down_ready = sem("down_ready")
    down_free = sem("down_free")
    y_ready = sem("y_ready")
    stored = sem("y_stored")

    def turn_slots():
        return [divmod(s, FC) for s in range(2, FC + 2)]

    def sync(sp):
        y = k.y.rearrange("b (t p) d -> p b t d", p=P)
        with sp.Fori(0, B) as b:
            sp.wait_ge(y_ready, T * (b + 1))
            sp.dma_start(y[:, bass.ds(b, 1)].rearrange("p o t d -> p (o t) d"),
                         k.res[:, bass.ds(T * b, T), :]).then_inc(stored, 16)
        sp.wait_ge(stored, 16 * B)

    def gate_up(pe, b, m):
        for i, w in enumerate((k.gT, k.uT)):
            product(pe, gu_bank[BANK[m]][:, S * i:S * (i + 1)], lambda p, c: w[p][:, c, P * m:P * (m + 1)],
                    lambda p, c: k.xnT[p][:, c, bass.ds(S * b, S)], range(C))

    def tensor(pe):
        def first(b, m):
            n = FC * b + m
            if not isinstance(n, int) or n >= 2:
                pe.wait_ge(full_ready, n - 1)
                gate_up(pe, b, m)
            pe.matmul(share_bank[BANK[m]], k.expand[:, P * m:P * (m + 1)], k.wT[:, bass.ds(S * b, S)],
                      start=True, stop=True).then_inc(gu_ready, 1)

        def second(b, m):
            pe.wait_ge(h_ready, FC * b + m + 1)
            if m == 0:
                pe.wait_ge(down_free, b + 1)
            for t in range(T):
                mm = product(pe, down_bank[t], lambda p, c: h[p][:, c, P * t:P * (t + 1)],
                             lambda p, c: k.dT[p][:, c, :], [m], first=m == 0, last=m == FC - 1)
            if m == FC - 1:
                mm.then_inc(down_ready, 1)

        pe.wait_ge(k.wt_ready, 1)
        first(0, 0)
        first(0, 1)
        with pe.Fori(0, B - 1) as b:
            for i, m in turn_slots():
                first(b + i, m)
                second(b, FC * i + m - 2)
        for i, m in turn_slots():
            if i == 0:
                first(B - 1, m)
            second(B - 1, FC * i + m - 2)

    def scalar(act):
        def gate(b, m):
            act.wait_ge(gu_ready, FC * b + m + 1)
            nc.scalar.activation(tanh[BANK[m]][:], gu_bank[BANK[m]][:, 0:S], ACT.Tanh, scale=0.5
                                 ).then_inc(tanh_ready, 1)

        def hi_part(b, m):
            act.wait_ge(full_ready, FC * b + m + 1)
            nc.scalar.activation(h[0][:, m, :], full[BANK[m]][:], ACT.Copy).then_inc(h_hi, 1)

        gate(0, 0)
        gate(0, 1)
        hi_part(0, 0)
        with act.Fori(0, B - 1) as b:
            for i, m in turn_slots():
                gate(b + i, m)
                hi_part(b + (FC * i + m - 1) // FC, (m - 1) % FC)
        for m in range(2, FC):
            gate(B - 1, m)
            hi_part(B - 1, m - 1)
        hi_part(B - 1, FC - 1)

    def vector(dve):
        dve.sem_inc(down_free, 1)
        V = nc.vector

        def gate(b, m):
            n, i = FC * b + m, BANK[m]
            dve.wait_ge(tanh_ready, n + 1)
            V.scalar_tensor_tensor(gated[:], tanh[i][:], 1.0, gu_bank[i][:, 0:S], ALU.add, ALU.mult
                                   ).then_inc(gated_ready, 1)
            dve.wait_ge(gated_ready, n + 1)
            V.tensor_tensor(gated_up[:], gu_bank[i][:, S:2 * S], gated[:], ALU.mult).then_inc(up_ready, 1)
            dve.wait_ge(up_ready, n + 1)
            V.tensor_tensor(full[i][:], share_bank[i], gated_up[:], ALU.mult).then_inc(full_ready, 1)

        def lo_part(b, m):
            dve.wait_ge(h_hi, FC * b + m + 1)
            V.tensor_tensor(h[1][:, m, :], full[BANK[m]][:], h[0][:, m, :].bitcast(F32), ALU.subtract
                            ).then_inc(h_ready, 1)

        def output(b):
            dve.wait_ge(down_ready, b + 1)
            for t in range(T):
                res = k.res[:, bass.ds(T * b + t, 1), :].rearrange("p o d -> p (o d)")
                V.tensor_tensor(res, down_bank[t], res, ALU.add).then_inc(y_ready, 1)
            dve.wait_ge(y_ready, T * (b + 1))
            dve.sem_inc(down_free, 1)

        gate(0, 0)
        gate(0, 1)
        lo_part(0, 0)
        with dve.Fori(0, B - 1) as b:
            for i, m in turn_slots():
                gate(b + i, m)
                lo_part(b + (FC * i + m - 1) // FC, (m - 1) % FC)
            output(b)
        for m in range(2, FC):
            gate(B - 1, m)
            lo_part(B - 1, m - 1)
        lo_part(B - 1, FC - 1)
        output(B - 1)

    k.gate_up = gate_up
    return Programs(sync, None, tensor, scalar, vector)


def build(nc, x, ctx_4096, wq, wk, wv, wo, gate_w, u, g, d, y):
    with ExitStack() as ctx:
        k = Plan()
        k.x, k.ctx, k.wq, k.wk, k.wv, k.wo, k.gate_w, k.u, k.g, k.d, k.y = x, ctx_4096, wq, wk, wv, wo, gate_w, u, g, d, y
        psum = ctx.enter_context(nc.psum_tensor("psum", [P, 8, 512], F32))
        k.bank = psum
        fixed = k_base(nc)

        def at(name, shape, offset, dt=F32):
            return nc.alloc_sbuf_tensor_at(name, shape, dt, offset=fixed + offset)

        k.at = at
        k.ident = at("ident", [P, P], AT_IDENT)
        k.eps = at("eps", [P, 1], AT_EPS)
        k.expert_no = at("expert_no", [P, E], AT_NUMBERS)
        k.g_raw, k.u_raw = (at(f"{n}_raw", [P, FC, D], AT_ATT + 14 * KB * i) for i, n in enumerate(("g", "u")))
        k.att = [at(f"att_{n}", [P, B * C, S], AT_ATT + 16 * KB * i, F32R) for i, n in enumerate(("hi", "lo"))]
        k.wo_raw = at("wo_raw", [P, C, D], AT_WO)
        k.wo_part = [at(f"wo_{n}", [P, C, D], AT_WO_PARTS + 8 * KB * i, F32R) for i, n in enumerate(("hi", "lo"))]
        shapes = [P, C, F], [P, C, F], [P, FC, D]
        k.gT_full, k.uT_full, k.dT_full = (at(f"{n}T_full", shape, AT_TURNED + 14 * KB * i)
                                           for i, (n, shape) in enumerate(zip("gud", shapes)))
        k.gT, k.uT, k.dT = ([at(f"{n}T_{p}", shape, start + 14 * KB * i, F32R)
                             for p, start in (("hi", AT_V), ("lo", AT_TURNED))]
                            for i, (n, shape) in enumerate(zip("gud", shapes)))
        k.gateT = [at(f"gateT_{n}", [P, C, P], AT_GATE + 2 * KB * i, F32R) for i, n in enumerate(("hi", "lo"))]
        k.expand = at("expand", [P, F], AT_EXPAND, F32R)
        k.res = at("res", [P, B * S // P, D], AT_RES)
        k.xnT = [at(f"xnT_{n}", [P, C, B * S], AT_XN + 16 * KB * i, F32R) for i, n in enumerate(("hi", "lo"))]
        k.wT = at("wT", [P, B * S], AT_WT, F32R)
        k.v = at("v", [P, 2 * B, TILES, REP * HD], AT_V)
        k.k_dram = nc.dram_tensor("k_parts", [2, GROUPS * HD, SK], F32, kind="Internal").ap()
        k.q_dram = nc.dram_tensor("q_parts", [2, B * D, S], F32, kind="Internal").ap()
        k.sums_dram, k.inv_dram = (nc.dram_tensor(n, [FOUR * REP, S], F32, kind="Internal").ap()
                                   for n in ("sums", "inv_sums_dram"))
        k.sem = lambda name: ctx.enter_context(nc.semaphore(name))
        k.gu_loaded = ctx.enter_context(nc.semaphore("gu_loaded"))
        k.x_loaded = ctx.enter_context(nc.semaphore("x_loaded"))
        project(nc, k)
        stages = attend(nc, k), mix(nc, k), experts(nc, k)
        block = ctx.enter_context(nc.Block())

        @block.sync
        def _(sp):
            for stage in stages:
                if stage.sync:
                    stage.sync(sp)

        @block.gpsimd
        def _(pool):
            for stage in stages:
                if stage.gpsimd:
                    stage.gpsimd(pool)

        @block.tensor
        def _(pe):
            for stage in stages:
                stage.tensor(pe)

        @block.scalar
        def _(act):
            for stage in stages:
                stage.scalar(act)

        @block.vector
        def _(dve):
            for stage in stages:
                stage.vector(dve)


_INS = ['x', 'ctx_4096', 'L0_xattn_Wq', 'L0_xattn_Wk', 'L0_xattn_Wv', 'L0_xattn_Wo', 'L0_ffn_gate_w', 'L0_ffn_u',
        'L0_ffn_g', 'L0_ffn_d']
_OUTS = [((B, S, D), 'float32')]


def kernel(**inputs):
    import numpy as _np
    import concourse.bacc as _bacc
    from concourse import mybir as _mybir
    from concourse.bass_utils import run_bass_kernel_spmd as _run

    nc = _bacc.Bacc("TRN2", target_bir_lowering=False, num_devices=1)
    arrays, args = {}, []
    for name in _INS:
        a = _np.ascontiguousarray(inputs[name])
        arrays[f"in_{name}_dram"] = a
        args.append(nc.dram_tensor(f"in_{name}_dram", a.shape, _mybir.dt.from_np(a.dtype), kind="ExternalInput").ap())
    for i, (shape, dtype) in enumerate(_OUTS):
        dt = _mybir.dt.from_np(_np.dtype(dtype))
        args.append(nc.dram_tensor(f"out_{i}_dram", shape, dt, kind="ExternalOutput").ap())
    build(nc, *args)
    r = _run(nc, [arrays], core_ids=[0])
    got = tuple(r.results[0][f"out_{i}_dram"] for i in range(len(_OUTS)))
    return got[0]
```

```python
from contextlib import ExitStack

import concourse.bass as bass
from concourse import mybir

F32 = mybir.dt.float32
F32R = mybir.dt.float32r
U32 = mybir.dt.uint32
ACT = mybir.ActivationFunctionType
ALU = mybir.AluOpType
AX = mybir.AxisListType

P = 128
B, S, D = 4, 256, 512
SK = 1601
C = D // P
HEADS, KV, HD = 32, 8, 16
REP = HEADS // KV
QC = REP * S
TILES = (SK + P - 1) // P
LAST = SK - (TILES - 1) * P
GROUPS = B * KV
NQ = QC // P
PIECES = 4
PIECE = 402
STARTS = [min(i * (PIECE - 2), SK - PIECE) for i in range(PIECES)]
UNITS = NQ * PIECES
FOUR = 4
E, INTER = 16, 56
F = E * INTER
FC = F // P
EPS = 1e-5
CONSTS = 9
PARTS = ((0, 0), (0, 1), (1, 0))
ZROW, MROW = 64, 96
SROWS = MROW + 2

KB = 1024
AT_IDENT, AT_EPS, AT_NUMBERS = 0, KB // 2, KB // 2 + 64
AT_ATT = KB
AT_WO = 33 * KB
AT_TURNED = 41 * KB
AT_V = 83 * KB
AT_WORK = 109 * KB
AT_EARLY_END = AT_WORK + 23 * KB
AT_RES = AT_WORK + 17 * KB
AT_XN = AT_RES + 16 * KB
AT_WT = AT_XN + 32 * KB
AT_GATE = 181 * KB
AT_WO_PARTS = 185 * KB
AT_GATE_RAW = 201 * KB
AT_EXPAND = 204 * KB


class Plan:
    pass


class Programs:

    def __init__(self, sync, gpsimd, tensor, scalar, vector):
        self.sync, self.gpsimd, self.tensor, self.scalar, self.vector = sync, gpsimd, tensor, scalar, vector


def k_base(nc):
    return (nc.sbuf_base + 63) // 64 * 64


def product(pe, out, lhsT, rhs, chunks, first=True, last=True, between=None):
    steps = [(p, q, c) for p, q in PARTS for c in chunks]
    for i, (p, q, c) in enumerate(steps):
        mm = pe.matmul(out, lhsT(p, c), rhs(q, c), start=first and i == 0,
                       stop=last and i == len(steps) - 1)
        if between and (i + 1) % len(chunks) == 0:
            between()
    return mm


def project(nc, k):
    base = [k_base(nc) + AT_EARLY_END]

    def sb(name, shape, dt):
        size = 4
        for n in shape[1:]:
            size *= n
        t = nc.alloc_sbuf_tensor_at(name, shape, dt, offset=base[0])
        base[0] += (size + 63) // 64 * 64
        return t

    def sem(name):
        return k.sem(name)

    wraw = sb("wraw", [P, C, D + 2 * P], F32)
    w = [sb(f"w{n}", [P, C, D + 2 * P], F32R) for n in ("hi", "lo")]
    tok = [sb(f"tok{i}", [P, 4, D], F32) for i in range(2)]
    tokT = [[k.at(f"tokT{n}{i}", [P, C, 4 * P], AT_TURNED + 8 * KB * (2 * i + j), F32R)
             for j, n in enumerate(("hi", "lo"))] for i in range(2)]
    out = [[sb(f"out{n}{i}", [P, 4 * P], F32R) for n in ("hi", "lo")] for i in range(2)]
    vT = k.at("vT", [P, 4 * P], AT_WO - 2 * KB)
    stats = sb("stats", [P, 8, 6], F32)
    mean_var = sb("mean_var", [P, 8, 2], F32)
    std = sb("std", [P, 8], F32)
    rstd = sb("rstd", [P, 8], F32)
    assert base[0] - k_base(nc) <= AT_EXPAND
    band = [k.at(f"band{i}", [2 * E, F], AT_TURNED + 32 * KB + 4 * KB * i) for i in range(2)]
    turn_bank = [k.bank[:, i, :] for i in range(3)]
    kq_bank = [k.bank[:, 4 + i, :] for i in range(2)]
    vt_bank, v_bank = k.bank[:, 6, :], k.bank[:, 7, :]

    w_loaded = [sem(f"w_loaded{i}") for i in range(3)]
    w_ready = sem("w_ready")
    w_hi_done = sem("w_hi_done")
    id_zero = sem("id_zero")
    id_ready = sem("id_ready")
    tok_loaded = [sem(f"tok_loaded{i}") for i in range(2)]
    stats_ready = sem("stats_ready")
    var_ready = sem("var_ready")
    eps_ready = sem("eps_ready")
    std_ready = sem("std_ready")
    rstd_ready = sem("rstd_ready")
    ln_done = sem("ln_done")
    turned = sem("turned")
    turn_hi = sem("turn_hi")
    turn_lo = sem("turn_lo")
    kq_ready = sem("kq_ready")
    kq_hi = sem("kq_hi")
    kq_lo = sem("kq_lo")
    stored = [sem(f"stored{i}") for i in range(2)]
    vt_ready = sem("vt_ready")
    vt_copied = sem("vt_copied")
    v_ready = sem("v_ready")
    v_free = sem("v_free")
    consts = sem("consts")

    x_tok = k.x.rearrange("b s d -> (b s) d")
    QU = 8
    X_TILES = B * S // P

    def tiles(r):
        return 4 if r < 3 else 1

    def rows(r):
        return P if r < 3 else LAST

    def bank_no(r, j):
        return (4 * r + j) % 3

    FIRST_TILES, LAST_TILE = range(3), range(3, 4)

    def following(b, r):
        return b + (r + 1) // 4, (r + 1) % 4

    def is_first(b, r):
        return isinstance(b, int) and (b, r) == (0, 0)

    def first_tile(b, r):
        return 0 if is_first(b, r) else X_TILES + TILES * b + 4 * r

    def product_no(b, r):
        return 0 if is_first(b, r) else QU + 4 * b + r

    def x_tile(u, j):
        return 4 * (u + 1) + j

    def q_no(u, m):
        return 1 + 4 * u + m

    def sync(sp):
        def load_x(u):
            if u == 1:
                sp.wait_ge(turned, 4)
            sp.dma_start(tok[1 - u][:], x_tok[512 * u:512 * u + 512, :].rearrange("(t p) d -> p t d", p=P)
                         ).then_inc(tok_loaded[1 - u], 16)

        def load(b, r):
            if isinstance(b, int) and b == 0 and r < 2:
                if r == 1:
                    sp.wait_ge(turned, x_tile(1, 0))
            elif r < 2:
                sp.wait_ge(turned, first_tile(b - 1, r + 2) + tiles(r + 2))
            else:
                sp.wait_ge(turned, X_TILES + TILES * b + 4 * (r - 1))
            src = k.ctx[bass.ds(b, 1), 512 * r:512 * r + P * (tiles(r) - 1) + rows(r), :]
            sp.dma_start(tok[r % 2][0:rows(r), 0:tiles(r), :],
                         src.rearrange("o (t p) d -> p (o t) d", p=rows(r))).then_inc(tok_loaded[r % 2], 16)

        def store_k(b, r):
            sp.wait_ge(kq_lo, product_no(b, r) + 1)
            n = P * (tiles(r) - 1) + rows(r)
            for part in range(2):
                sp.dma_start(k.k_dram[part, bass.ds(P * b, P), 512 * r:512 * r + n],
                             out[r % 2][part][:, 0:n].bitcast(F32)).then_inc(stored[r % 2], 16)

        def store_q(u):
            for m in range(C):
                n = q_no(u, m)
                sp.wait_ge(kq_lo, n + 1)
                for part in range(2):
                    dst = k.q_dram[part, 2 * D * u:2 * D * (u + 1), :].rearrange("(b n) q -> n b q", b=2)
                    sp.dma_start(dst[P * m:P * (m + 1)], out[n % 2][part][:].bitcast(F32)
                                 .rearrange("p (b q) -> p b q", b=2)).then_inc(stored[n % 2], 16)

        def load_weights(i, w_dram, lo, hi):
            sp.dma_start(wraw[:, :, lo:hi], w_dram.rearrange("(c p) n -> p c n", p=P)).then_inc(w_loaded[i], 16)

        load(0, 0)
        load_weights(0, k.wv, D + P, D + 2 * P)
        load_weights(1, k.wk, D, D + P)
        load_x(0)
        load_weights(2, k.wq, 0, D)
        load_x(1)
        store_k(0, 0)
        load(0, 1)
        store_q(0)
        load(0, 2)
        store_q(1)
        load(0, 3)

        def batch(b):
            for r in range(4):
                load(b, r)
                if r < 3:
                    store_k(b - 1, r + 1)
            store_k(b, 0)

        with sp.Fori(1, B - 1) as b:
            batch(b)
        for i in range(2):
            sp.wait_ge(stored[i], 32 * (QU // 2 + 2))
        for i in range(2):
            k.load(sp, 0, i)
        batch(B - 1)
        for raw, w_dram in ((k.g_raw, k.g), (k.u_raw, k.u)):
            sp.dma_start(raw[:], w_dram.rearrange("(m p) d -> p m d", p=P)).then_inc(k.gu_loaded, 16)
        for r in range(1, 4):
            store_k(B - 1, r)

    def gpsimd(pool):
        nc.gpsimd.memset(k.ident[:], 0.0).then_inc(id_zero, 1)
        pool.wait_ge(id_zero, 1)
        nc.gpsimd.affine_select(out=k.ident[:], in_=k.ident[:], compare_op=ALU.not_equal, fill=1.0, base=0,
                                pattern=[[-1, P]], channel_multiplier=1).then_inc(id_ready, 1)
        for i, (lo, hi) in enumerate(((D + P, D + 2 * P), (D, D + P), (0, D))):
            pool.wait_ge(w_loaded[i], 16)
            nc.gpsimd.tensor_copy(w[0][:, :, lo:hi], wraw[:, :, lo:hi]).then_inc(w_hi_done, 1)
            pool.wait_ge(w_hi_done, i + 1)
            nc.gpsimd.tensor_tensor(w[1][:, :, lo:hi], wraw[:, :, lo:hi], w[0][:, :, lo:hi].bitcast(F32),
                                    ALU.subtract).then_inc(w_ready, 1)
        pool.wait_ge(w_ready, 3)
        for i in range(2):
            k.fix_rows(pool, i)
        nc.gpsimd.memset(k.expand[:].bitcast(F32), 0.0).then_inc(consts, 1)
        nc.gpsimd.iota(k.expert_no[:], [[1, E]], base=0, channel_multiplier=0,
                       allow_small_or_imprecise_dtypes=True).then_inc(consts, 1)
        for i in range(2):
            nc.gpsimd.memset(band[i][:], 0.5).then_inc(consts, 1)
        pool.wait_ge(consts, 4)
        for i in range(2):
            nc.gpsimd.affine_select(out=band[i][:], in_=band[i][:], compare_op=ALU.is_ge, fill=0.0,
                                    base=INTER * E * i, pattern=[[1, F]], channel_multiplier=-INTER
                                    ).then_inc(consts, 1)
            pool.wait_ge(consts, 5 + 2 * i)
            nc.gpsimd.affine_select(out=band[i][:], in_=band[i][:], compare_op=ALU.is_ge, fill=0.0,
                                    base=INTER - 1 - INTER * E * i, pattern=[[-1, F]], channel_multiplier=INTER
                                    ).then_inc(consts, 1)
            pool.wait_ge(consts, 6 + 2 * i)
        nc.gpsimd.tensor_tensor(k.expand[0:2 * E, :], band[0][:], band[1][:], ALU.add).then_inc(consts, 1)

    def tensor(pe):
        early = iter(range(UNITS))

        def row():
            step = next(early, None)
            if step is not None:
                k.rows_step_pe(pe, 0, 0, step)

        def turn_ctx(b, r, some, between=None):
            if some[0] == 0:
                pe.wait_ge(tok_loaded[r % 2], 16 if is_first(b, r) else 16 * (2 + 2 * b + r // 2))
                if r == 0 and not is_first(b, r) or isinstance(b, int) and (b, r) == (0, 1):
                    pe.wait_ge(turn_lo, first_tile(b, r))
            np_ = rows(r)
            for j in some[:tiles(r)]:
                t = first_tile(b, r) + j
                if not isinstance(t, int) or t > 2:
                    pe.wait_ge(turn_lo, t - 2)
                for c in range(C):
                    mm = pe.transpose(turn_bank[bank_no(r, j)][:, P * c:P * c + np_],
                                      tok[r % 2][0:np_, j, P * c:P * (c + 1)], k.ident[0:np_, 0:np_])
                mm.then_inc(turned, 1)
                if between and j % 2 == 1:
                    between()

        def turn_x(u, some):
            for j in some:
                t = x_tile(u, j)
                pe.wait_ge(ln_done, 4 * u + j + 1)
                pe.wait_ge(turn_lo, t - 2)
                for c in range(C):
                    mm = pe.transpose(turn_bank[t % 3][:, P * c:P * (c + 1)], tok[1 - u][:, j, P * c:P * (c + 1)],
                                      k.ident[:])
                mm.then_inc(turned, 1)

        def q_of(u, turn_next):
            pe.wait_ge(turn_lo, x_tile(u + 1, 0))
            pe.wait_ge(w_ready, 3)
            for m in range(C):
                n = q_no(u, m)
                if n >= 2:
                    pe.wait_ge(kq_lo, n - 1)
                product(pe, kq_bank[n % 2], lambda p, c: w[p][:, c, P * m:P * (m + 1)],
                        lambda p, c: tokT[1 - u][p][:, c, :], range(C)).then_inc(kq_ready, 1)
                if m > 0 and m < C - 1:
                    turn_next((FIRST_TILES, LAST_TILE)[m - 1])

        def unit(b, r, then, between=None):
            if then:
                turn_ctx(*then, FIRST_TILES, between)
            n, np_ = tiles(r), rows(r)
            pe.wait_ge(turn_lo, first_tile(b, r) + n)
            cols = P * (n - 1) + np_ + np_ % 2
            product(pe, vt_bank[:, 0:cols], lambda p, c: w[p][:, c, D + P:D + 2 * P],
                    lambda p, c: tokT[r % 2][p][:, c, 0:cols], range(C), between=between).then_inc(vt_ready, 1)
            if is_first(b, r):
                turn_x(0, FIRST_TILES)
            if then and then[1] < 3:
                turn_ctx(*then, LAST_TILE, between)
            if not is_first(b, r):
                pe.wait_ge(kq_lo, product_no(b, r) - 1)
            product(pe, kq_bank[r % 2][:, 0:cols], lambda p, c: w[p][:, c, D:D + P],
                    lambda p, c: tokT[r % 2][p][:, c, 0:cols], range(C), between=between).then_inc(kq_ready, 1)
            if is_first(b, r):
                turn_x(0, LAST_TILE)
            pe.wait_ge(vt_copied, 4 * b + r + 1)
            pe.wait_ge(v_free, 4 * b + r + 1)
            for j in range(n):
                mm = pe.transpose(v_bank[0:np_, P * j:P * (j + 1)], vT[:, P * j:P * j + np_], k.ident[:])
            mm.then_inc(v_ready, 1)

        pe.wait_ge(id_ready, 1)
        turn_ctx(0, 0, range(4))
        pe.wait_ge(w_ready, 2)
        unit(0, 0, None)
        q_of(0, lambda some: turn_x(1, some))
        q_of(1, lambda some: turn_ctx(0, 1, some))
        for r in range(1, 4):
            unit(0, r, following(0, r))
        with pe.Fori(1, B - 1) as b:
            for r in range(4):
                unit(b, r, following(b, r))
        for r in range(4):
            unit(B - 1, r, following(B - 1, r) if r < 3 else None, row)
        for _ in range(UNITS):
            row()

    def scalar(act):
        act.sem_inc(v_free, 1)

        def turn_part(slot, j, t, np_, bank):
            act.wait_ge(turned, t + 1)
            src = turn_bank[bank].rearrange("p (c n) -> p c n", c=C)[:, :, 0:np_]
            nc.scalar.activation(tokT[slot][0][:, :, P * j:P * j + np_], src, ACT.Copy).then_inc(turn_hi, 1)

        def turn_x(u, some):
            if u == 1:
                act.wait_ge(kq_ready, 1)
            for j in some:
                turn_part(1 - u, j, x_tile(u, j), P, x_tile(u, j) % 3)

        def turn_ctx(b, r, some):
            if isinstance(b, int) and (b, r) == (0, 1):
                act.wait_ge(kq_ready, q_no(1, 0))
            elif some[0] == 0 and not is_first(b, r):
                act.wait_ge(kq_ready, QU + 4 * b + r - 1)
            for j in some[:tiles(r)]:
                turn_part(r % 2, j, first_tile(b, r) + j, rows(r), bank_no(r, j))

        def q_of(u, turn_next):
            for m in range(C):
                n = q_no(u, m)
                act.wait_ge(kq_ready, n + 1)
                if n >= 2:
                    act.wait_ge(stored[n % 2], 32 * (n // 2))
                nc.scalar.activation(out[n % 2][0][:], kq_bank[n % 2], ACT.Copy).then_inc(kq_hi, 1)
                if m > 0 and m < C - 1:
                    turn_next((FIRST_TILES, LAST_TILE)[m - 1])

        def unit(b, r, then):
            if then:
                turn_ctx(*then, FIRST_TILES)
            n, np_ = tiles(r), rows(r)
            cols = P * (n - 1) + np_
            act.wait_ge(vt_ready, 4 * b + r + 1)
            nc.scalar.activation(vT[:, 0:cols], vt_bank[:, 0:cols], ACT.Copy).then_inc(vt_copied, 1)
            if is_first(b, r):
                turn_x(0, FIRST_TILES)
            if then and then[1] < 3:
                turn_ctx(*then, LAST_TILE)
            act.wait_ge(kq_ready, product_no(b, r) + 1)
            if not is_first(b, r):
                act.wait_ge(stored[r % 2], 32 * (QU // 2 + 2 * b + r // 2))
            nc.scalar.activation(out[r % 2][0][:, 0:cols], kq_bank[r % 2][:, 0:cols], ACT.Copy).then_inc(kq_hi, 1)
            if is_first(b, r):
                turn_x(0, LAST_TILE)
            act.wait_ge(v_ready, 4 * b + r + 1)
            dst = k.v[0:np_, bass.ds(2 * b, 2), 4 * r:4 * r + n, :].rearrange("p h t d -> p t h d")
            src = v_bank[0:np_, 0:P * n].rearrange("p (t h d) -> p t h d", t=n, h=2)
            nc.scalar.activation(dst, src, ACT.Copy).then_inc(v_free, 1)

        def std_of(u):
            act.wait_ge(var_ready, 4 * (u + 1))
            nc.scalar.activation(std[:, 4 * u:4 * u + 4], mean_var[:, 4 * u:4 * u + 4, 1], ACT.Sqrt,
                                 bias=k.eps[:]).then_inc(std_ready, 1)

        act.wait_ge(eps_ready, 1)
        turn_ctx(0, 0, range(4))
        std_of(0)
        unit(0, 0, None)
        std_of(1)
        q_of(0, lambda some: turn_x(1, some))
        q_of(1, lambda some: turn_ctx(0, 1, some))
        for r in range(1, 4):
            unit(0, r, following(0, r))
        with act.Fori(1, B - 1) as b:
            for r in range(4):
                unit(b, r, following(b, r))
        for r in range(4):
            unit(B - 1, r, following(B - 1, r) if r < 3 else None)

    def vector(dve):
        dve.sem_inc(k.rows_free, 3)

        def turn_part(slot, j, t, np_, bank):
            dve.wait_ge(turn_hi, t + 1)
            src = turn_bank[bank].rearrange("p (c n) -> p c n", c=C)[:, :, 0:np_]
            hi, lo = (tokT[slot][p][:, :, P * j:P * j + np_] for p in range(2))
            nc.vector.tensor_tensor(lo, src, hi.bitcast(F32), ALU.subtract).then_inc(turn_lo, 1)

        early = iter(range(UNITS))

        def row():
            step = next(early, None)
            if step is not None:
                k.rows_step_dve(dve, 0, 0, step)

        def turn_ctx(b, r, some, between=None):
            for j in some[:tiles(r)]:
                turn_part(r % 2, j, first_tile(b, r) + j, rows(r), bank_no(r, j))
                if between and j % 2 == 1:
                    between()

        def kq_part(n, slot, cols):
            dve.wait_ge(kq_hi, n + 1)
            nc.vector.tensor_tensor(out[slot][1][:, 0:cols], kq_bank[slot][:, 0:cols],
                                    out[slot][0][:, 0:cols].bitcast(F32), ALU.subtract).then_inc(kq_lo, 1)

        def q_of(u, turn_next):
            for m in range(C):
                kq_part(q_no(u, m), q_no(u, m) % 2, 4 * P)
                if m > 0 and m < C - 1:
                    turn_next((FIRST_TILES, LAST_TILE)[m - 1])

        def unit(b, r, then, between=None):
            for some in (FIRST_TILES, LAST_TILE):
                if then and (some[0] == 0 or then[1] < 3):
                    turn_ctx(*then, some, between)
                if between:
                    for _ in PARTS:
                        between()
            kq_part(product_no(b, r), r % 2, P * (tiles(r) - 1) + rows(r))

        nc.vector.memset(k.eps[:], EPS).then_inc(eps_ready, 1)

        def normalise(u):
            x = tok[1 - u]
            dve.wait_ge(tok_loaded[1 - u], 16 * (u + 1))
            for j in range(4):
                nc.vector.bn_stats(stats[:, 4 * u + j, :], x[:, j, :]).then_inc(stats_ready, 1)
            dve.wait_ge(stats_ready, 4 * (u + 1))
            for j in range(4):
                nc.vector.bn_aggr(mean_var[:, 4 * u + j, :], stats[:, 4 * u + j, :]).then_inc(var_ready, 1)
            dve.wait_ge(std_ready, u + 1)
            nc.vector.reciprocal(rstd[:, 4 * u:4 * u + 4], std[:, 4 * u:4 * u + 4]).then_inc(rstd_ready, 1)
            dve.wait_ge(rstd_ready, u + 1)
            for j in range(4):
                nc.vector.tensor_scalar(x[:, j, :], x[:, j, :], mean_var[:, 4 * u + j, 0:1],
                                        rstd[:, 4 * u + j:4 * u + j + 1], ALU.subtract, ALU.mult
                                        ).then_inc(ln_done, 1)

        def turn_x(u, some):
            for j in some:
                turn_part(1 - u, j, x_tile(u, j), P, x_tile(u, j) % 3)

        turn_ctx(0, 0, range(4))
        normalise(0)
        turn_x(0, FIRST_TILES)
        unit(0, 0, None)
        turn_x(0, LAST_TILE)
        normalise(1)
        q_of(0, lambda some: turn_x(1, some))
        q_of(1, lambda some: turn_ctx(0, 1, some))
        for r in range(1, 4):
            unit(0, r, following(0, r))
        with dve.Fori(1, B - 1) as b:
            for r in range(4):
                unit(b, r, following(b, r))
        for r in range(4):
            unit(B - 1, r, following(B - 1, r) if r < 3 else None, row)
        for _ in range(UNITS):
            row()

    k.consts, k.stored, k.v_free, k.kq_lo, k.v_done = consts, stored, v_free, kq_lo, v_ready
    k.all_stored, k.all_v, k.all_kq = 32 * (QU // 2 + 2 * B), 4 * B, QU + 4 * B
    return Programs(sync, gpsimd, tensor, scalar, vector)


def attend(nc, k):
    base = [k_base(nc) + AT_WORK]

    def sb(name, shape, dt):
        size = 4
        for n in shape[1:]:
            size *= n
        t = nc.alloc_sbuf_tensor_at(name, shape, dt, offset=base[0])
        base[0] += (size + 63) // 64 * 64
        return t

    def sem(name):
        return k.sem(name)

    ks, qs = [None] * FOUR, [None] * FOUR

    def operands(i):
        ks[i] = sb(f"ks{i}", [P, SK], F32R)
        qs[i] = sb(f"qs{i}", [P, QC], F32R)

    operands(0)
    piece_max = [sb(f"piece_max{i}", [P, UNITS], F32) for i in range(2)]
    neg_max = [sb(f"neg_max{i}", [P, NQ], F32) for i in range(2)]
    max_hi = [sb(f"max_hi{i}", [NQ, P], F32R) for i in range(2)]
    max_lo = [sb(f"max_lo{i}", [NQ, P], F32R) for i in range(2)]
    operands(1)
    assert base[0] - k_base(nc) <= AT_EARLY_END
    assert base[0] - k_base(nc) >= AT_RES
    operands(2)
    assert base[0] - k_base(nc) >= AT_XN
    operands(3)
    vg = [sb(f"vg{i}", [P, TILES, 2 * HD], F32) for i in range(2)]
    probs = [sb(f"probs{i}", [P, QC], F32) for i in range(FOUR)]
    pv = [sb(f"pv{i}", [P, S], F32) for i in range(2)]
    sums = sb("sums", [P, FOUR * QC // P], F32)
    inv_sums = sb("inv_sums", [P, FOUR * QC // P], F32)
    inv = sb("inv", [P, 2, S], F32)
    att = sb("att", [P, 2, S], F32)
    tick = sb("tick", [P, 1], F32)
    assert base[0] - k_base(nc) <= AT_GATE
    d_raw = k.at("d_raw", [P, C, F], AT_WO_PARTS)
    gate_raw = k.at("gate_raw", [E, D], AT_GATE_RAW)
    early_bank = [k.bank[:, i, :] for i in (3, 0, 1, 2)]
    score_bank = [k.bank[:, 2 * i:2 * i + 2, :].rearrange("p b n -> p (b n)") for i in range(2)]
    pv_bank = k.bank[:, 4, 0:S]
    row_bank = [k.bank[:, 5 + i, :] for i in range(3)]

    fixed_rows = sem("fixed_rows")
    loaded = [sem(f"qk_loaded{i}") for i in range(FOUR)]
    max_loaded = [sem(f"max_loaded{i}") for i in range(FOUR)]
    rows_ready = sem("rows_ready")
    rows_free = sem("rows_free")
    max_ready = sem("max_ready")
    max_split = sem("max_split")
    scores_ready = sem("scores_ready")
    probs_ready = sem("probs_ready")
    v_ready = sem("vg_ready")
    pv_done = sem("pv_done")
    pv_free = sem("pv_free")
    pv_moved = [sem(f"pv_moved{i}") for i in range(2)]
    sums_loaded = sem("sums_loaded")
    inv_ready = sem("inv_ready")
    inv_stored = sem("inv_stored")
    inv_loaded = sem("inv_loaded")
    att_ready = sem("att_ready")
    att_hi, att_lo = sem("att_hi"), sem("att_lo")
    d_loaded, gate_loaded, wo_loaded = sem("d_loaded"), sem("gate_loaded"), sem("wo_loaded")
    turned = sem("w_turned")
    copied = [sem(f"w_copied{i}") for i in range(2)]
    gate_lo = sem("gate_lo")
    wo_hi, wo_lo = sem("wo_hi"), sem("wo_lo")
    w_hi, w_lo = sem("w_hi"), sem("w_lo")

    TURNS = GROUPS // FOUR
    MOVES = 16 * (REP + 1)
    FIXED = 3 * FOUR + 4
    AHEAD = TILES + 6
    ONE_BANK = 8 + 8 + 6

    def keys(t):
        return P if t < TILES - 1 else LAST

    def units(part):
        return range(UNITS * part // TILES, UNITS * (part + 1) // TILES)

    def row_steps(g, i, t, last):
        ahead, part = divmod(t + AHEAD - TILES, TILES)
        g, i = g + 1 + ahead, i + 1 + ahead
        steps = []
        for u in units(part):
            if u == 3 and not (last and i > FOUR):
                steps.append((g - 1, i - 1, "max"))
            if not (last and i >= FOUR):
                steps.append((g, i, u))
        return steps

    def index(g, step, last=False):
        if step == "max":
            return (UNITS + 1) * (g + 1) + (2 if not last else -1)
        if isinstance(g, int) and g == 0:
            return step
        return (UNITS + 1) * g - 1 + step + (step >= 3)

    def bank_of(g, step):
        if isinstance(g, int) and g == 0 and step != "max":
            return early_bank[0 if step < ONE_BANK else 1 + (step - ONE_BANK) % 3]
        return row_bank[index(0 if step == "max" or (isinstance(g, int) and g == 0) else 3, step) % 3]

    def first_rows(do):
        for part in range(AHEAD - TILES):
            for u in units(part):
                if u == 3:
                    do(0, 0, "max")
                do(1, 1, u)

    W_UNITS = 3 * FC + 1

    def raw_blocks(n):
        m = n % FC
        if n < 2 * FC:
            return [(k.g_raw, k.u_raw)[n // FC][:, m, P * c:P * (c + 1)] for c in range(C)]
        if n < 3 * FC:
            return [d_raw[:, c, P * m:P * (m + 1)] for c in range(C)]
        return [gate_raw[:, P * c:P * (c + 1)] for c in range(C)]

    def turned_home(n):
        m = n % FC
        if n < 2 * FC:
            return (k.gT_full, k.uT_full)[n // FC][:, :, P * m:P * (m + 1)]
        if n < 3 * FC:
            return k.dT_full[:, m, :].rearrange("p (c n) -> p c n", c=C)
        return k.gateT[0][:, :, 0:E]

    def width(n):
        return P if n < 3 * FC else E

    def turned_bank(n):
        return k.bank[:, n % 4, 0:C * width(n)]

    def turn_slots(last):
        return [divmod(s, TILES) for s in range(1, FOUR * TILES + (0 if last else 1))]

    def stage1_done(engine):
        engine.wait_ge(k.v_done, k.all_v)
        engine.wait_ge(k.v_free, k.all_v + 1)
        engine.wait_ge(k.kq_lo, k.all_kq)
        for i in range(2):
            engine.wait_ge(k.stored[i], k.all_stored)

    def fix_rows(pool, i):
        nc.gpsimd.memset(ks[i][ZROW:MROW, :].bitcast(F32), 0.0).then_inc(fixed_rows, 1)
        nc.gpsimd.memset(ks[i][MROW:SROWS, :].bitcast(F32), 1.0).then_inc(fixed_rows, 1)
        nc.gpsimd.memset(qs[i][ZROW:MROW, :].bitcast(F32), 0.0).then_inc(fixed_rows, 1)
        pool.wait_ge(fixed_rows, 3 * (i + 1))

    def gpsimd(pool):
        stage1_done(pool)
        pool.wait_ge(k.consts, CONSTS)
        for i in range(2, FOUR):
            fix_rows(pool, i)
        for i in range(2):
            nc.gpsimd.memset(vg[i][:, :, HD:], 1.0).then_inc(fixed_rows, 1)
        for p in range(2):
            nc.gpsimd.memset(k.gateT[p][:, :, E:].bitcast(F32), 0.0).then_inc(fixed_rows, 1)

        def copy(h, i):
            for rows, t0, t1 in ((P, 0, TILES - 1), (LAST, TILES - 1, TILES)):
                src = k.v[0:rows, bass.ds(h + i // FOUR, 1), t0:t1, HD * (i % FOUR):HD * (i % FOUR + 1)]
                nc.gpsimd.tensor_copy(vg[i % 2][0:rows, t0:t1, 0:HD],
                                      src.rearrange("p o t d -> p (o t) d")).then_inc(v_ready, 1)

        def after():
            nc.gpsimd.tensor_tensor(tick[:], k.eps[:], k.eps[:], ALU.add)

        def divide(h):
            here = [x[:, bass.ds(2 * h, 2), :] for x in k.att]
            pool.wait_ge(att_lo, h + 1)
            pool.wait_ge(inv_loaded, 32 * (h + 1))
            after()
            nc.gpsimd.tensor_tensor(att[:], here[1].bitcast(F32), inv[:], ALU.mult).then_inc(att_ready, 1)
            pool.wait_ge(att_ready, h + 2)
            nc.gpsimd.tensor_copy(here[0], att[:]).then_inc(att_hi, 1)
            pool.wait_ge(att_hi, h + 1)
            after()
            nc.gpsimd.tensor_tensor(here[1], att[:], here[0].bitcast(F32), ALU.subtract).then_inc(att_lo, 1)

        pool.sem_inc(att_ready, 1)
        pool.sem_inc(att_lo, 1)
        copy(0, 0)
        copy(0, 1)
        pool.wait_ge(wo_loaded, 16)
        for i in range(2):
            pool.wait_ge(copied[i], (3 * FC + 1 - i) // 2)
        nc.gpsimd.tensor_copy(k.wo_part[0][:], k.wo_raw[:]).then_inc(wo_hi, 1)
        pool.wait_ge(wo_hi, 1)
        nc.gpsimd.tensor_tensor(k.wo_part[1][:], k.wo_raw[:], k.wo_part[0][:].bitcast(F32), ALU.subtract
                                ).then_inc(wo_lo, 1)

        def copy_next(h, i):
            pool.wait_ge(pv_done, TILES * (FOUR * h + i + 1))
            copy(h, i + 2)

        for i in range(FOUR):
            copy_next(0, i)
        with pool.Fori(1, TURNS - 1) as h:
            for i in range(FOUR):
                copy_next(h, i)
                if i == 2:
                    divide(h - 1)
        for i in range(FOUR - 2):
            copy_next(TURNS - 1, i)
        divide(TURNS - 2)
        divide(TURNS - 1)

    def load(sp, h, i):
        g = FOUR * h + i
        for part in range(2):
            sp.dma_start(ks[i][2 * HD * part:2 * HD * (part + 1), :].bitcast(F32),
                         k.k_dram[part, bass.ds(HD * g, HD), :].partition_broadcast(2)
                         ).then_inc(loaded[i], 16)
            src = k.q_dram[part, bass.ds(REP * HD * g, REP * HD), :].rearrange("(h d) q -> d h q", h=REP)
            for row in (HD * part, HD * (part + 2)):
                sp.dma_start(qs[i][row:row + HD, :].bitcast(F32).rearrange("d (h q) -> d h q", h=REP),
                             src).then_inc(loaded[i], 16)

    def sync(sp):
        def put_max(g, i, last=False):
            sp.wait_ge(rows_free, index(g, "max", last) + 1 + 3)
            for n, src in enumerate((max_hi, max_lo)):
                row = MROW + n
                sp.dma_start(qs[i % FOUR][row:row + 1, :].bitcast(F32).rearrange("o (j q) -> o j q", j=NQ),
                             src[i % 2][:].bitcast(F32)).then_inc(max_loaded[i % FOUR], 16)

        def put_pv(h, i):
            sp.wait_ge(pv_free, FOUR * h + i + 2)
            for j in range(REP):
                row = 64 * (i % 2) + HD * j
                sp.dma_start(k.att[1][row:row + HD, bass.ds(2 * h + i // 2, 1), :].bitcast(F32)
                             .rearrange("p o q -> p (o q)"), pv[i % 2][32 * j:32 * j + HD, :]
                             ).then_inc(pv_moved[i % 2], 16)
            if i == 0:
                sp.wait_ge(sums_loaded, 16 * (h + 1))
            sp.dma_start(k.sums_dram[REP * i:REP * (i + 1), :], pv[i % 2][HD::32, :]).then_inc(pv_moved[i % 2], 16)

        def load_sums(h):
            for i in range(2):
                sp.wait_ge(pv_moved[i], MOVES * (2 * h + 3))
            sp.wait_ge(inv_ready, h + 1)
            sp.dma_start(sums[:], k.sums_dram.rearrange("(a n) (b q) -> (a n b) q", a=2, b=8)
                         ).then_inc(sums_loaded, 16)

        def replicate(h):
            sp.wait_ge(inv_ready, h + 2)
            sp.wait_ge(att_ready, h + 1)
            sp.dma_start(k.inv_dram.rearrange("(a n) (b q) -> (a n b) q", a=2, b=8), inv_sums[:]
                         ).then_inc(inv_stored, 16)
            sp.wait_ge(inv_stored, 16 * (h + 1))
            for c in range(2):
                src = k.inv_dram[8 * c:8 * (c + 1), :].unsqueeze(1).broadcast_to([8, HD, S])
                sp.dma_start(inv[:, c, :], src).then_inc(inv_loaded, 16)

        stage1_done(sp)
        sp.dma_start(d_raw[:], k.d.rearrange("(c p) f -> p c f", p=P)).then_inc(d_loaded, 16)
        sp.dma_start(gate_raw[:], k.gate_w).then_inc(gate_loaded, 16)
        load(sp, 0, 2)
        load(sp, 0, 3)
        sp.dma_start(k.wo_raw[:], k.wo.rearrange("(c p) n -> p c n", p=P)).then_inc(wo_loaded, 16)
        put_max(0, 0)

        def group(h, i, first):
            put_max(FOUR * h + i + 1, i + 1)
            sp.wait_ge(scores_ready, TILES * (FOUR * h + i + 1))
            load(sp, h + 1, i)
            if i == 1 and not first:
                replicate(h - 1)
            put_pv(h, i)

        for i in range(FOUR):
            group(0, i, True)
        load_sums(0)
        with sp.Fori(1, TURNS - 1) as h:
            for i in range(FOUR):
                group(h, i, False)
            load_sums(h)
        for i in range(FOUR):
            if i < FOUR - 1:
                put_max(GROUPS - FOUR + i + 1, i + 1, last=i == FOUR - 2)
            if i == 1:
                replicate(TURNS - 2)
            if i == FOUR - 1:
                sp.wait_ge(scores_ready, TILES * (GROUPS - 1) + 1)
                sp.dma_start(k.res[:], k.x.rearrange("b (t p) d -> p (b t) d", p=P)).then_inc(k.x_loaded, 16)
            put_pv(TURNS - 1, i)
        load_sums(TURNS - 1)
        replicate(TURNS - 1)
        sp.wait_ge(inv_loaded, 32 * TURNS)

    def rows_step_pe(pe, g, i, step, last=False):
        bank = bank_of(g, step)
        if step == "max":
            pe.wait_ge(max_ready, g + 1)
        if isinstance(g, int) and g == 0 and step != "max" and step < ONE_BANK:
            pe.wait_ge(rows_free, step + 3)
        else:
            pe.wait_ge(rows_free, index(g, step, last) + 1)
        if step == "max":
            pe.transpose(bank[0:NQ, 0:P], neg_max[i % 2][:], k.ident[:]).then_inc(rows_ready, 1)
            return
        if isinstance(g, int) and g < 2 and step == 0:
            pe.wait_ge(fixed_rows, 3 * (g + 1))
        if step == 0:
            pe.wait_ge(loaded[i % FOUR], 24 * (g - i % FOUR) + 96)
        j, piece = divmod(step, PIECES)
        pe.matmul(bank[:, 0:PIECE], qs[i % FOUR][0:MROW, P * j:P * (j + 1)],
                  ks[i % FOUR][0:MROW, STARTS[piece]:STARTS[piece] + PIECE],
                  start=True, stop=True).then_inc(rows_ready, 1)

    def tensor(pe):
        def rows_step(g, i, step, last=False):
            rows_step_pe(pe, g, i, step, last)

        def scores(h, i, t):
            if t == 0:
                pe.wait_ge(max_loaded[i % FOUR], 32 * (h + i // FOUR + 1))
            s = TILES * i + t
            for half in range(2):
                mm = pe.matmul(score_bank[s % 2][0:keys(t), 512 * half:512 * (half + 1)],
                               ks[i % FOUR][0:SROWS, P * t:P * t + keys(t)],
                               qs[i % FOUR][0:SROWS, 512 * half:512 * (half + 1)], start=True, stop=True)
            mm.then_inc(scores_ready, 1)

        def p_v(h, i, t):
            g, s = FOUR * h + i, TILES * i + t
            pe.wait_ge(probs_ready, TILES * g + t + 1)
            if t == 0:
                pe.wait_ge(v_ready, 2 * (g + 1))
                pe.wait_ge(pv_free, g + 1)
            for j in range(REP):
                mm = pe.matmul(pv_bank[32 * j:32 * (j + 1), :], vg[i % 2][0:keys(t), t, :],
                               probs[s % FOUR][0:keys(t), S * j:S * (j + 1)],
                               start=t == 0, stop=t == TILES - 1)
            mm.then_inc(pv_done, 1)

        def slot(h, i, t, last):
            scores(h, i, t)
            steps = row_steps(FOUR * h + i, i, t, last)
            for g, ii, step in steps[:1]:
                rows_step(g, ii, step, last and ii == FOUR - 1)
            p_v(h, *divmod(TILES * i + t - 1, TILES))
            for g, ii, step in steps[1:]:
                rows_step(g, ii, step, last and ii == FOUR - 1)

        def turn_weights(n):
            for at, loaded_sem, count in ((0, k.gu_loaded, 32), (2 * FC, d_loaded, 16), (3 * FC, gate_loaded, 16)):
                if n == at:
                    pe.wait_ge(loaded_sem, count)
            if n >= 4:
                pe.wait_ge(copied[n % 2], n // 2 - 1)
            w = width(n)
            for c, blk in enumerate(raw_blocks(n)):
                mm = pe.transpose(turned_bank(n)[:, w * c:w * (c + 1)], blk, k.ident[0:w, 0:w])
            mm.then_inc(turned, 1)

        weights = iter(range(W_UNITS))

        def row_and_weights(g, i, step):
            n = next(weights, None)
            if n is not None:
                turn_weights(n)
            rows_step(g, i, step)

        pe.wait_ge(k.kq_lo, k.all_kq)
        pe.wait_ge(k.v_free, k.all_v + 1)
        pe.wait_ge(rows_free, UNITS + 3)
        first_rows(row_and_weights)
        for n in weights:
            turn_weights(n)
        pe.wait_ge(fixed_rows, FIXED)
        for i in range(2):
            pe.wait_ge(copied[i], (W_UNITS + 1 - i) // 2)
        pe.wait_ge(gate_lo, 1)
        scores(0, 0, 0)
        for g, ii, step in row_steps(0, 0, 0, False):
            rows_step(g, ii, step)
        with pe.Fori(0, TURNS - 1) as h:
            for i, t in turn_slots(False):
                slot(h, i, t, False)
        for i, t in turn_slots(True):
            slot(TURNS - 1, i, t, True)
        p_v(TURNS - 1, FOUR - 1, TILES - 1)

    def scalar(act):
        act.sem_inc(pv_free, 1)
        for i in range(2):
            act.sem_inc(pv_moved[i], MOVES)
        act.wait_ge(k.consts, CONSTS)
        for n in range(0, W_UNITS, 2):
            act.wait_ge(turned, n + 1)
            nc.scalar.activation(turned_home(n), turned_bank(n).rearrange("p (c n) -> p c n", c=C), ACT.Copy
                                 ).then_inc(copied[0], 1)

        def exponential(h, i, t):
            s = TILES * i + t
            act.wait_ge(scores_ready, TILES * FOUR * h + s + 1)
            nc.scalar.activation(probs[s % FOUR][0:keys(t), :], score_bank[s % 2][0:keys(t), :], ACT.Exp,
                                 scale=HD ** -0.5).then_inc(probs_ready, 1)

        def take_pv(h, i):
            g = FOUR * h + i
            act.wait_ge(pv_done, TILES * (g + 1))
            act.wait_ge(pv_moved[i % 2], MOVES * (2 * h + i // 2 + 1))
            nc.scalar.activation(pv[i % 2][:], pv_bank, ACT.Copy).then_inc(pv_free, 1)

        exponential(0, 0, 0)
        with act.Fori(0, TURNS - 1) as h:
            for i, t in turn_slots(False):
                exponential(h, i, t)
                if t == 0:
                    take_pv(h, i - 1)
        for i, t in turn_slots(True):
            exponential(TURNS - 1, i, t)
            if t == 0:
                take_pv(TURNS - 1, i - 1)
        take_pv(TURNS - 1, FOUR - 1)

    def invert(dve, turns):
        dve.wait_ge(sums_loaded, 16 * turns + 16)
        nc.vector.reciprocal(inv_sums[:], sums[:]).then_inc(inv_ready, 1)

    def rows_step_dve(dve, g, i, step, last=False):
        bank, n = bank_of(g, step), index(g, step, last)
        dve.wait_ge(rows_ready, n + 1)
        if step == "max":
            nc.vector.tensor_copy(max_hi[i % 2][:], bank[0:NQ, 0:P]).then_inc(max_split, 1)
            dve.wait_ge(max_split, g + 1)
            nc.vector.tensor_tensor(max_lo[i % 2][:], bank[0:NQ, 0:P], max_hi[i % 2][:].bitcast(F32),
                                    ALU.subtract).then_inc(rows_free, 1)
            return
        nc.vector.tensor_reduce(piece_max[i % 2][:, step:step + 1], bank[:, 0:PIECE], AX.X, ALU.max
                                ).then_inc(rows_free, 1)
        if step == UNITS - 1:
            dve.wait_ge(rows_free, n + 1 + 3)
            nc.vector.tensor_reduce(neg_max[i % 2][:], piece_max[i % 2][:].rearrange("p (j c) -> p j c", c=PIECES),
                                    AX.X, ALU.max, negate=True).then_inc(max_ready, 1)

    def vector(dve):
        def rows_step(g, i, step, last=False):
            rows_step_dve(dve, g, i, step, last)

        weights = iter(range(W_UNITS))

        def copy_weights(n):
            src = turned_bank(n).rearrange("p (c n) -> p c n", c=C)
            if n % 2:
                dve.wait_ge(turned, n + 1)
                nc.vector.tensor_copy(turned_home(n), src).then_inc(copied[1], 1)

        def row_and_weights(g, i, step):
            n = next(weights, None)
            if n is not None:
                copy_weights(n)
            rows_step(g, i, step)

        dve.wait_ge(k.v_done, k.all_v)
        dve.wait_ge(k.consts, CONSTS)
        first_rows(row_and_weights)
        for n in weights:
            copy_weights(n)
        n = W_UNITS - 1
        assert n % 2
        dve.wait_ge(copied[1], W_UNITS // 2)
        nc.vector.tensor_tensor(k.gateT[1][:, :, 0:E], turned_bank(n).rearrange("p (c n) -> p c n", c=C),
                                k.gateT[0][:, :, 0:E].bitcast(F32), ALU.subtract).then_inc(gate_lo, 1)
        stage1_done(dve)
        nc.vector.memset(sums[:], 1.0).then_inc(sums_loaded, 16)
        for g, ii, step in row_steps(0, 0, 0, False):
            rows_step(g, ii, step)
        with dve.Fori(0, TURNS - 1) as h:
            for i, t in turn_slots(False):
                for g, ii, step in row_steps(FOUR * h + i, i, t, False):
                    rows_step(g, ii, step)
                if (i, t) == (0, 8):
                    invert(dve, h)
        for i, t in turn_slots(True):
            for g, ii, step in row_steps(FOUR * (TURNS - 1) + i, i, t, True):
                rows_step(g, ii, step, ii == FOUR - 1)
            if (i, t) == (0, 8):
                invert(dve, TURNS - 1)
        dve.wait_ge(scores_ready, TILES * (GROUPS - 2))
        dve.wait_ge(v_ready, 2 * GROUPS)
        for i, (w, parts) in enumerate(((k.gT_full, k.gT), (k.uT_full, k.uT), (k.dT_full, k.dT))):
            if i == 2:
                dve.wait_ge(max_loaded[FOUR - 1], 32 * TURNS)
            nc.vector.tensor_copy(parts[0][:], w[:]).then_inc(w_hi, 1)
            dve.wait_ge(w_hi, i + 1)
            nc.vector.tensor_tensor(parts[1][:], w[:], parts[0][:].bitcast(F32), ALU.subtract).then_inc(w_lo, 1)

    k.att_lo, k.wo_lo, k.w_lo, k.pv_free, k.pv_moved = att_lo, wo_lo, w_lo, pv_free, pv_moved
    k.row_pieces = rows_free, index(GROUPS - 1, UNITS - 1, True) + 1 + 3
    k.all_moved = MOVES * (2 * TURNS + 1)
    k.load, k.fix_rows, k.rows_free = load, fix_rows, rows_free
    k.rows_step_pe, k.rows_step_dve = rows_step_pe, rows_step_dve
    k.invert_last = lambda dve: invert(dve, TURNS)
    return Programs(sync, gpsimd, tensor, scalar, vector)


def mix(nc, k):

    def sem(name):
        return k.sem(name)

    T = S // P
    NT = B * T
    room = {"small": AT_WO, "more": AT_GATE_RAW}

    def tiny(name, shape, dt=F32, where="small"):
        size = 4
        for n in shape[1:]:
            size *= n
        t = k.at(name, shape, room[where], dt)
        room[where] += (size + 63) // 64 * 64
        return t

    xn = [tiny(f"xn{t}", [P, D]) for t in range(2)]
    stats, mean_var = tiny("stats3", [P, NT, 6]), tiny("mean_var3", [P, NT, 2])
    std, rstd = tiny("std3", [P, NT]), tiny("rstd3", [P, NT])
    logits, top_logit = tiny("logits", [P, NT, E]), tiny("top_logit", [P, NT, 8])
    exps, total, inv_total = tiny("exps", [P, NT, E]), tiny("total", [P, NT]), tiny("inv_total", [P, NT])
    prob, top, top_at = tiny("prob", [P, NT, E]), tiny("top", [P, NT, 8]), tiny("top_at", [P, NT, 8], U32)
    two, inv_two = tiny("two", [P, NT]), tiny("inv_two", [P, NT])
    share, at_f = tiny("share", [P, NT, 2]), tiny("at_f", [P, NT, 2])
    w1, w2, w = (tiny(f"w_{n}", [P, NT, E], where="more") for n in ("first", "second", "both"))
    wparts = tiny("wparts", [P, NT, 2 * E], where="more")
    assert room["small"] <= AT_TURNED and room["more"] <= AT_EXPAND
    ltT = k.at("ltT", [E, B * S], AT_ATT)

    wo_bank = [k.bank[:, i, :] for i in range(T)]
    turn_bank = [k.bank[:, 2 + i, :] for i in range(2)]
    lt_bank = [k.bank[:, 4 + i, 0:S] for i in range(2)]
    logit_bank = k.bank[:, 3, 0:NT * E]
    wt_bank = k.bank[:, 6:8, :].rearrange("p b n -> p (b n)")

    wo_ready = sem("wo_ready")
    added = sem("added")
    stats_ready = sem("stats3_ready")
    var_ready = sem("var3_ready")
    std_ready = sem("std3_ready")
    rstd_ready = sem("rstd3_ready")
    xn_ready = sem("xn_ready")
    turned = sem("xn_turned")
    turn_hi, turn_lo = sem("xn_hi"), sem("xn_lo")
    lt_ready, lt_copied = sem("lt_ready"), sem("lt_copied")
    logit_turned, logit_ready = sem("logit_turned"), sem("logit_ready")
    less_top = sem("less_top")
    exp_ready = sem("exp_ready")
    step = sem("router_step")
    w_split = sem("w_split")
    wt_turned, wt_ready = sem("wt_turned"), sem("wt_ready")
    wt_zero = sem("wt_zero")

    def gpsimd(pool):
        pool.wait_ge(k.att_lo, GROUPS // FOUR + 1)
        nc.gpsimd.memset(k.wT[:].bitcast(F32), 0.0).then_inc(wt_zero, 1)

    def tensor(pe):
        def project_out(t):
            b, col = t // T, P * (t % T)
            if t % T == 0:
                pe.wait_ge(k.att_lo, 2 * (b + 1) + 1)
            if t >= 2:
                pe.wait_ge(added, t - 1)
            product(pe, wo_bank[t % 2], lambda p, c: k.att[p][:, C * b + c, col:col + P],
                    lambda p, c: k.wo_part[p][:, c, :], range(C)).then_inc(wo_ready, 1)

        def turn(t):
            pe.wait_ge(xn_ready, t + 1)
            if t >= 2:
                pe.wait_ge(turn_lo, t - 1)
            for c in range(C):
                mm = pe.transpose(turn_bank[t % 2][:, P * c:P * (c + 1)], xn[t % 2][:, P * c:P * (c + 1)],
                                  k.ident[:])
            mm.then_inc(turned, 1)

        def logits_of(b):
            pe.wait_ge(turn_lo, T * (b + 1))
            if b == 0:
                pe.wait_ge(k.pv_free, GROUPS + 1)
                pe.wait_ge(*k.row_pieces)
            if b >= 2:
                pe.wait_ge(lt_copied, b - 1)
            product(pe, lt_bank[b % 2], lambda p, c: k.gateT[p][:, c, :],
                    lambda p, c: k.xnT[p][:, c, S * b:S * (b + 1)], range(C)).then_inc(lt_ready, 1)

        pe.wait_ge(k.wo_lo, 1)
        project_out(0)
        project_out(1)
        for t in range(NT):
            if t + 2 < NT:
                project_out(t + 2)
            turn(t)
            if t >= T and t % T == T - 1:
                logits_of(t // T - 1)
        logits_of(B - 1)
        for b in range(B):
            pe.wait_ge(lt_copied, b + 1)
            for t in range(T * b, T * (b + 1)):
                mm = pe.transpose(logit_bank[:, E * t:E * (t + 1)], ltT[:, P * t:P * (t + 1)], k.ident[0:E, 0:E])
        mm.then_inc(logit_turned, 1)
        pe.wait_ge(k.w_lo, 3)
        for m in range(2):
            k.gate_up(pe, 0, m)
        pe.wait_ge(w_split, 1)
        for t in range(NT):
            mm = pe.transpose(wt_bank[0:2 * E, P * t:P * (t + 1)], wparts[:, t, :], k.ident[:])
        mm.then_inc(wt_turned, 1)

    def scalar(act):
        def std_of(t):
            act.wait_ge(var_ready, t + 1)
            nc.scalar.activation(std[:, t:t + 1], mean_var[:, t, 1:2], ACT.Sqrt, bias=k.eps[:]).then_inc(std_ready, 1)

        std_of(0)
        for t in range(NT):
            if t + 1 < NT:
                std_of(t + 1)
            act.wait_ge(turned, t + 1)
            nc.scalar.activation(k.xnT[0][:, :, P * t:P * (t + 1)],
                                 turn_bank[t % 2].rearrange("p (c n) -> p c n", c=C), ACT.Copy
                                 ).then_inc(turn_hi, 1)
            b = t // T - 1
            if b >= 0 and t % T == T - 1:
                act.wait_ge(lt_ready, b + 1)
                nc.scalar.activation(ltT[:, S * b:S * (b + 1)], lt_bank[b % 2][0:E, :], ACT.Copy
                                     ).then_inc(lt_copied, 1)
        b = B - 1
        act.wait_ge(lt_ready, b + 1)
        nc.scalar.activation(ltT[:, S * b:S * (b + 1)], lt_bank[b % 2][0:E, :], ACT.Copy).then_inc(lt_copied, 1)
        act.wait_ge(logit_turned, 1)
        nc.scalar.activation(logits[:].rearrange("p t e -> p (t e)"), logit_bank, ACT.Copy).then_inc(logit_ready, 1)
        act.wait_ge(less_top, 1)
        nc.scalar.activation(exps[:], logits[:], ACT.Exp).then_inc(exp_ready, 1)
        act.wait_ge(wt_turned, 1)
        act.wait_ge(wt_zero, 1)
        nc.scalar.activation(k.wT[0:2 * E, :], wt_bank[0:2 * E, :], ACT.Copy).then_inc(wt_ready, 1)

    def vector(dve):
        dve.wait_ge(k.x_loaded, 16)
        dve.wait_ge(k.consts, CONSTS)
        dve.wait_ge(k.wo_lo, 1)
        V = nc.vector

        def add(t):
            res = k.res[:, t, :]
            dve.wait_ge(wo_ready, t + 1)
            V.tensor_tensor(res, wo_bank[t % 2], res, ALU.add).then_inc(added, 1)
            dve.wait_ge(added, t + 1)
            V.bn_stats(stats[:, t, :], res).then_inc(stats_ready, 1)
            dve.wait_ge(stats_ready, t + 1)
            V.bn_aggr(mean_var[:, t, :], stats[:, t, :]).then_inc(var_ready, 1)

        def normalise(t):
            dve.wait_ge(std_ready, t + 1)
            V.reciprocal(rstd[:, t:t + 1], std[:, t:t + 1]).then_inc(rstd_ready, 1)
            dve.wait_ge(rstd_ready, t + 1)
            if t >= 2:
                dve.wait_ge(turned, t - 1)
            V.tensor_scalar(xn[t % 2][:], k.res[:, t, :], mean_var[:, t, 0:1], rstd[:, t:t + 1], ALU.subtract,
                            ALU.mult).then_inc(xn_ready, 1)

        def split(t):
            if t == 0:
                for i in range(2):
                    dve.wait_ge(k.pv_moved[i], k.all_moved)
            dve.wait_ge(turn_hi, t + 1)
            hi, lo = (k.xnT[p][:, :, P * t:P * (t + 1)] for p in range(2))
            V.tensor_tensor(lo, turn_bank[t % 2].rearrange("p (c n) -> p c n", c=C), hi.bitcast(F32),
                            ALU.subtract).then_inc(turn_lo, 1)

        add(0)
        add(1)
        normalise(0)
        k.invert_last(dve)
        for t in range(NT):
            if t + 1 < NT:
                normalise(t + 1)
            if t + 2 < NT:
                add(t + 2)
            split(t)
        done = [0]

        def mark(ins):
            done[0] += 1
            ins.then_inc(step, 1)

        def marked():
            dve.wait_ge(step, done[0])

        def over(column):
            return column.broadcast_to([P, NT, E])

        dve.wait_ge(logit_ready, 1)
        for t in range(NT):
            mark(V.max(top_logit[:, t, :], logits[:, t, :]))
        marked()
        V.tensor_tensor(logits[:], logits[:], over(top_logit[:, :, 0:1]), ALU.subtract).then_inc(less_top, 1)
        dve.wait_ge(exp_ready, 1)
        mark(V.tensor_reduce(total[:], exps[:], AX.X, ALU.add))
        marked()
        mark(V.reciprocal(inv_total[:], total[:]))
        marked()
        mark(V.tensor_tensor(prob[:], exps[:], over(inv_total[:].unsqueeze(2)), ALU.mult))
        marked()
        for t in range(NT):
            mark(V.max(top[:, t, :], prob[:, t, :]))
        marked()
        for t in range(NT):
            mark(V.max_index(top_at[:, t, :], top[:, t, :], prob[:, t, :]))
        mark(V.tensor_tensor(two[:], top[:, :, 0], top[:, :, 1], ALU.add))
        marked()
        mark(V.reciprocal(inv_two[:], two[:]))
        mark(V.tensor_copy(at_f[:], top_at[:, :, 0:2]))
        marked()
        mark(V.tensor_tensor(share[:], top[:, :, 0:2], inv_two[:].unsqueeze(2).broadcast_to([P, NT, 2]), ALU.mult))
        numbers = k.expert_no[:].unsqueeze(1).broadcast_to([P, NT, E])
        for dst, n in ((w1, 0), (w2, 1)):
            mark(V.tensor_tensor(dst[:], numbers, over(at_f[:, :, n:n + 1]), ALU.is_equal))
        marked()
        for dst, n in ((w1, 0), (w2, 1)):
            mark(V.tensor_tensor(dst[:], dst[:], over(share[:, :, n:n + 1]), ALU.mult))
        marked()
        mark(V.tensor_tensor(w[:], w1[:], w2[:], ALU.add))
        marked()
        mark(V.tensor_copy(wparts[:, :, 0:E].bitcast(F32R), w[:]))
        marked()
        V.tensor_tensor(wparts[:, :, E:], w[:], wparts[:, :, 0:E], ALU.subtract).then_inc(w_split, 1)

    k.wt_ready = wt_ready
    return Programs(None, gpsimd, tensor, scalar, vector)


def experts(nc, k):

    def sem(name):
        return k.sem(name)

    T = S // P
    h = [k.at(f"h_{n}", [P, FC, S], AT_ATT + 7 * KB * i, F32R) for i, n in enumerate(("hi", "lo"))]
    work = AT_ATT + 14 * KB
    BANK = (0, 1, 0, 1, 0, 1, 2)
    tanh = [k.at(f"tanh{i}", [P, S], work + KB * i) for i in range(3)]
    gated = k.at("gated", [P, S], work + 3 * KB)
    gated_up = k.at("gated_up", [P, S], work + 4 * KB)
    full = [k.at(f"h_full{i}", [P, S], work + KB * (5 + i)) for i in range(3)]
    gu_bank = [k.bank[:, i, :] for i in range(3)]
    share_bank = [k.bank[:, 3 + i, 0:S] for i in range(3)]
    down_bank = [k.bank[:, 6 + t, :] for t in range(T)]

    gu_ready = sem("gu_ready")
    tanh_ready = sem("tanh_ready")
    gated_ready = sem("gated_ready")
    up_ready = sem("gated_up_ready")
    full_ready = sem("h_full_ready")
    h_hi = sem("h_hi")
    h_ready = sem("h_ready")
    down_ready = sem("down_ready")
    down_free = sem("down_free")
    y_ready = sem("y_ready")
    stored = sem("y_stored")

    def turn_slots():
        return [divmod(s, FC) for s in range(2, FC + 2)]

    def sync(sp):
        y = k.y.rearrange("b (t p) d -> p b t d", p=P)
        with sp.Fori(0, B) as b:
            sp.wait_ge(y_ready, T * (b + 1))
            sp.dma_start(y[:, bass.ds(b, 1)].rearrange("p o t d -> p (o t) d"),
                         k.res[:, bass.ds(T * b, T), :]).then_inc(stored, 16)
        sp.wait_ge(stored, 16 * B)

    def gate_up(pe, b, m):
        for i, w in enumerate((k.gT, k.uT)):
            product(pe, gu_bank[BANK[m]][:, S * i:S * (i + 1)], lambda p, c: w[p][:, c, P * m:P * (m + 1)],
                    lambda p, c: k.xnT[p][:, c, bass.ds(S * b, S)], range(C))

    def tensor(pe):
        def first(b, m):
            n = FC * b + m
            if not isinstance(n, int) or n >= 2:
                pe.wait_ge(full_ready, n - 1)
                gate_up(pe, b, m)
            pe.matmul(share_bank[BANK[m]], k.expand[:, P * m:P * (m + 1)], k.wT[:, bass.ds(S * b, S)],
                      start=True, stop=True).then_inc(gu_ready, 1)

        def second(b, m):
            pe.wait_ge(h_ready, FC * b + m + 1)
            if m == 0:
                pe.wait_ge(down_free, b + 1)
            for t in range(T):
                mm = product(pe, down_bank[t], lambda p, c: h[p][:, c, P * t:P * (t + 1)],
                             lambda p, c: k.dT[p][:, c, :], [m], first=m == 0, last=m == FC - 1)
            if m == FC - 1:
                mm.then_inc(down_ready, 1)

        pe.wait_ge(k.wt_ready, 1)
        pe.wait_ge(k.consts, CONSTS)
        first(0, 0)
        first(0, 1)
        with pe.Fori(0, B - 1) as b:
            for i, m in turn_slots():
                first(b + i, m)
                second(b, FC * i + m - 2)
        for i, m in turn_slots():
            if i == 0:
                first(B - 1, m)
            second(B - 1, FC * i + m - 2)

    def scalar(act):
        def gate(b, m):
            act.wait_ge(gu_ready, FC * b + m + 1)
            nc.scalar.activation(tanh[BANK[m]][:], gu_bank[BANK[m]][:, 0:S], ACT.Tanh, scale=0.5
                                 ).then_inc(tanh_ready, 1)

        def hi_part(b, m):
            act.wait_ge(full_ready, FC * b + m + 1)
            nc.scalar.activation(h[0][:, m, :], full[BANK[m]][:], ACT.Copy).then_inc(h_hi, 1)

        gate(0, 0)
        gate(0, 1)
        hi_part(0, 0)
        with act.Fori(0, B - 1) as b:
            for i, m in turn_slots():
                gate(b + i, m)
                hi_part(b + (FC * i + m - 1) // FC, (m - 1) % FC)
        for m in range(2, FC):
            gate(B - 1, m)
            hi_part(B - 1, m - 1)
        hi_part(B - 1, FC - 1)

    def vector(dve):
        dve.sem_inc(down_free, 1)
        V = nc.vector

        def gate(b, m):
            n, i = FC * b + m, BANK[m]
            dve.wait_ge(tanh_ready, n + 1)
            V.scalar_tensor_tensor(gated[:], tanh[i][:], 1.0, gu_bank[i][:, 0:S], ALU.add, ALU.mult
                                   ).then_inc(gated_ready, 1)
            dve.wait_ge(gated_ready, n + 1)
            V.tensor_tensor(gated_up[:], gu_bank[i][:, S:2 * S], gated[:], ALU.mult).then_inc(up_ready, 1)
            dve.wait_ge(up_ready, n + 1)
            V.tensor_tensor(full[i][:], share_bank[i], gated_up[:], ALU.mult).then_inc(full_ready, 1)

        def lo_part(b, m):
            dve.wait_ge(h_hi, FC * b + m + 1)
            V.tensor_tensor(h[1][:, m, :], full[BANK[m]][:], h[0][:, m, :].bitcast(F32), ALU.subtract
                            ).then_inc(h_ready, 1)

        def output(b):
            dve.wait_ge(down_ready, b + 1)
            for t in range(T):
                res = k.res[:, bass.ds(T * b + t, 1), :].rearrange("p o d -> p (o d)")
                V.tensor_tensor(res, down_bank[t], res, ALU.add).then_inc(y_ready, 1)
            dve.wait_ge(y_ready, T * (b + 1))
            dve.sem_inc(down_free, 1)

        gate(0, 0)
        gate(0, 1)
        lo_part(0, 0)
        with dve.Fori(0, B - 1) as b:
            for i, m in turn_slots():
                gate(b + i, m)
                lo_part(b + (FC * i + m - 1) // FC, (m - 1) % FC)
            output(b)
        for m in range(2, FC):
            gate(B - 1, m)
            lo_part(B - 1, m - 1)
        lo_part(B - 1, FC - 1)
        output(B - 1)

    k.gate_up = gate_up
    return Programs(sync, None, tensor, scalar, vector)


def build(nc, x, ctx_4096, wq, wk, wv, wo, gate_w, u, g, d, y):
    with ExitStack() as ctx:
        k = Plan()
        k.x, k.ctx, k.wq, k.wk, k.wv, k.wo, k.gate_w, k.u, k.g, k.d, k.y = x, ctx_4096, wq, wk, wv, wo, gate_w, u, g, d, y
        psum = ctx.enter_context(nc.psum_tensor("psum", [P, 8, 512], F32))
        k.bank = psum
        fixed = k_base(nc)

        def at(name, shape, offset, dt=F32):
            return nc.alloc_sbuf_tensor_at(name, shape, dt, offset=fixed + offset)

        k.at = at
        k.ident = at("ident", [P, P], AT_IDENT)
        k.eps = at("eps", [P, 1], AT_EPS)
        k.expert_no = at("expert_no", [P, E], AT_NUMBERS)
        k.g_raw, k.u_raw = (at(f"{n}_raw", [P, FC, D], AT_ATT + 14 * KB * i) for i, n in enumerate(("g", "u")))
        k.att = [at(f"att_{n}", [P, B * C, S], AT_ATT + 16 * KB * i, F32R) for i, n in enumerate(("hi", "lo"))]
        k.wo_raw = at("wo_raw", [P, C, D], AT_WO)
        k.wo_part = [at(f"wo_{n}", [P, C, D], AT_WO_PARTS + 8 * KB * i, F32R) for i, n in enumerate(("hi", "lo"))]
        shapes = [P, C, F], [P, C, F], [P, FC, D]
        k.gT_full, k.uT_full, k.dT_full = (at(f"{n}T_full", shape, AT_TURNED + 14 * KB * i)
                                           for i, (n, shape) in enumerate(zip("gud", shapes)))
        k.gT, k.uT, k.dT = ([at(f"{n}T_{p}", shape, start + 14 * KB * i, F32R)
                             for p, start in (("hi", AT_V), ("lo", AT_TURNED))]
                            for i, (n, shape) in enumerate(zip("gud", shapes)))
        k.gateT = [at(f"gateT_{n}", [P, C, P], AT_GATE + 2 * KB * i, F32R) for i, n in enumerate(("hi", "lo"))]
        k.expand = at("expand", [P, F], AT_EXPAND, F32R)
        k.res = at("res", [P, B * S // P, D], AT_RES)
        k.xnT = [at(f"xnT_{n}", [P, C, B * S], AT_XN + 16 * KB * i, F32R) for i, n in enumerate(("hi", "lo"))]
        k.wT = at("wT", [P, B * S], AT_WT, F32R)
        k.v = at("v", [P, 2 * B, TILES, REP * HD], AT_V)
        k.k_dram = nc.dram_tensor("k_parts", [2, GROUPS * HD, SK], F32, kind="Internal").ap()
        k.q_dram = nc.dram_tensor("q_parts", [2, B * D, S], F32, kind="Internal").ap()
        k.sums_dram, k.inv_dram = (nc.dram_tensor(n, [FOUR * REP, S], F32, kind="Internal").ap()
                                   for n in ("sums", "inv_sums_dram"))
        k.sem = lambda name: ctx.enter_context(nc.semaphore(name))
        k.gu_loaded = ctx.enter_context(nc.semaphore("gu_loaded"))
        k.x_loaded = ctx.enter_context(nc.semaphore("x_loaded"))
        stages = project(nc, k), attend(nc, k), mix(nc, k), experts(nc, k)
        block = ctx.enter_context(nc.Block())

        @block.sync
        def _(sp):
            for stage in stages:
                if stage.sync:
                    stage.sync(sp)

        @block.gpsimd
        def _(pool):
            for stage in stages:
                if stage.gpsimd:
                    stage.gpsimd(pool)

        @block.tensor
        def _(pe):
            for stage in stages:
                stage.tensor(pe)

        @block.scalar
        def _(act):
            for stage in stages:
                stage.scalar(act)

        @block.vector
        def _(dve):
            for stage in stages:
                stage.vector(dve)


_INS = ['x', 'ctx_4096', 'L0_xattn_Wq', 'L0_xattn_Wk', 'L0_xattn_Wv', 'L0_xattn_Wo', 'L0_ffn_gate_w', 'L0_ffn_u',
        'L0_ffn_g', 'L0_ffn_d']
_OUTS = [((B, S, D), 'float32')]


def kernel(**inputs):
    import numpy as _np
    import concourse.bacc as _bacc
    from concourse import mybir as _mybir
    from concourse.bass_utils import run_bass_kernel_spmd as _run

    nc = _bacc.Bacc("TRN2", target_bir_lowering=False, num_devices=1)
    arrays, args = {}, []
    for name in _INS:
        a = _np.ascontiguousarray(inputs[name])
        arrays[f"in_{name}_dram"] = a
        args.append(nc.dram_tensor(f"in_{name}_dram", a.shape, _mybir.dt.from_np(a.dtype), kind="ExternalInput").ap())
    for i, (shape, dtype) in enumerate(_OUTS):
        dt = _mybir.dt.from_np(_np.dtype(dtype))
        args.append(nc.dram_tensor(f"out_{i}_dram", shape, dt, kind="ExternalOutput").ap())
    build(nc, *args)
    r = _run(nc, [arrays], core_ids=[0])
    got = tuple(r.results[0][f"out_{i}_dram"] for i in range(len(_OUTS)))
    return got[0]
```
